# Optimizing a Trainium2 kernel written in Bass

```python
import numpy as np
import jax
import jax.numpy as jnp

def _softmax(x, axis=-1):
    return jax.nn.softmax(x, axis=axis)

def _gelu(x):
    return jax.nn.gelu(x, approximate=True)

def _silu(x):
    return jax.nn.silu(x)

def _sigmoid(x):
    return jax.nn.sigmoid(x)

def _layernorm(x, axis=-1, eps=1e-05):
    m = jnp.mean(x, axis=axis, keepdims=True)
    v = jnp.var(x, axis=axis, keepdims=True)
    return (x - m) / jnp.sqrt(v + eps)

def _scatter_add(tgt, idx, src, axis=0):
    return tgt.at[idx].add(src)

def _segment_sum(src, seg, n):
    return jax.ops.segment_sum(src, seg, n)
kernel_name = 'mk_perceiver_d1_seqx_r2_e95175'

def setup_inputs(seed: int=0):
    np.random.seed(seed)
    _w = jnp.asarray

    def _rec_inputs():
        import jax
        import jax.numpy as jnp
        _rk = jax.random.key(seed)
        x = 0.002226 + 0.9996 * jax.random.normal(jax.random.fold_in(_rk, 1), (8, 64, 512), jnp.float32)
        _lenS = 64 - jax.random.randint(jax.random.fold_in(_rk, 7), (8,), 0, max(1, 64 // 4) + 1, jnp.int32)
        _lenS2 = 1601 - jax.random.randint(jax.random.fold_in(_rk, 8), (8,), 0, max(1, 1601 // 4) + 1, jnp.int32)
        _ctx_1024P = jax.random.normal(jax.random.fold_in(_rk, 11), (8, 16, 512), jnp.float32)
        _ctx_1024c = jax.random.dirichlet(jax.random.fold_in(_rk, 511), 0.3 * jnp.ones((16,), jnp.float32), (8, 1601))
        _ctx_1024t = jnp.einsum('bsk,bkd->bsd', _ctx_1024c, _ctx_1024P)
        _ctx_1024t = _ctx_1024t * jax.lax.rsqrt(jnp.mean(jnp.square(_ctx_1024t)) + 1e-12) * 0.953939
        ctx_1024 = -7.10856e-05 + 0.999911 * (_ctx_1024t + 0.3 * jax.random.normal(jax.random.fold_in(_rk, 611), (8, 1601, 512), jnp.float32))
        _validS = jnp.arange(64)[None, :] < _lenS[:, None]
        _validS2 = jnp.arange(1601)[None, :] < _lenS2[:, None]
        _causal = jnp.tril(jnp.ones((64, 64), dtype=bool))
        mask_BxS2_bk0 = jnp.logical_not(jnp.broadcast_to(_validS2[:, :], (8, 1601)))
        return (x, ctx_1024, mask_BxS2_bk0)
    x, ctx_1024, mask_BxS2_bk0 = _rec_inputs()

    def _L0_xattn_setup():
        import jax, jax.numpy as jnp
        import numpy as np
        HEADS = 8
        DIM_HEAD = 64
        SCALE = DIM_HEAD ** (-0.5)
        LN_EPS = 1e-05
        NEG_INF = -1e+30

        def layernorm(x, gamma, beta):
            mu = jnp.mean(x, axis=-1, keepdims=True)
            var = jnp.var(x, axis=-1, keepdims=True)
            return (x - mu) * jax.lax.rsqrt(var + LN_EPS) * gamma + beta
        key = jax.random.key(seed)
        ks = jax.random.split(key, 8)
        b, f, n, d, inner = (8, 4096, 64, 512, HEADS * DIM_HEAD)
        x = jax.random.normal(ks[0], (b, f, d), dtype=jnp.float32)
        latents = jax.random.normal(ks[1], (b, n, d), dtype=jnp.float32)
        key_padding_mask = jax.random.randint(ks[2], (b, f), 0, 2) > 0
        s = 0.02
        return {'x': x, 'latents': latents, 'key_padding_mask': key_padding_mask, 'kv_gate': jnp.float32(-4.0), 'gamma_media': jnp.ones((d,), jnp.float32), 'beta_media': jnp.zeros((d,), jnp.float32), 'gamma_lat': jnp.ones((d,), jnp.float32), 'beta_lat': jnp.zeros((d,), jnp.float32), 'Wq': jax.random.normal(ks[3], (d, inner), jnp.float32) * s, 'Wk': jax.random.normal(ks[4], (d, inner), jnp.float32) * s, 'Wv': jax.random.normal(ks[5], (d, inner), jnp.float32) * s, 'Wout': jax.random.normal(ks[6], (inner, d), jnp.float32) * s}
    _L0_xattn_all = _L0_xattn_setup()
    _L0_xattn_in = {k: v for k, v in _L0_xattn_all.items() if k in ('kv_gate', 'gamma_media', 'beta_media', 'gamma_lat', 'beta_lat', 'Wq', 'Wk', 'Wv', 'Wout')}
    del _L0_xattn_all

    def _L0_attn_setup():
        import jax, jax.numpy as jnp
        import numpy as np
        key = jax.random.key(seed)
        x = jax.random.normal(key, (8, 1024, 512), dtype=jnp.float32)
        return {'x': x}
    _L0_attn_all = _L0_attn_setup()
    _L0_attn_in = {k: v for k, v in _L0_attn_all.items() if k in ()}
    del _L0_attn_all

    def _L0_ffn_setup():
        import jax, jax.numpy as jnp
        import numpy as np
        D_MODEL = 512
        N_EXPERTS = 8
        TOP_K = 2
        HIDDEN = 4 * D_MODEL
        key = jax.random.key(seed)
        ks = jax.random.split(key, 6)
        B, S = (2, 1024)
        x = jax.random.normal(ks[0], (B, S, D_MODEL), dtype=jnp.float32)
        shared_w1 = jax.random.normal(ks[1], (HIDDEN, D_MODEL), dtype=jnp.float32) * 0.02
        shared_w2 = jax.random.normal(ks[2], (D_MODEL, HIDDEN), dtype=jnp.float32) * 0.02
        experts_w1 = jax.random.normal(ks[3], (N_EXPERTS, HIDDEN, D_MODEL), dtype=jnp.float32) * 0.02
        experts_w2 = jax.random.normal(ks[4], (N_EXPERTS, D_MODEL, HIDDEN), dtype=jnp.float32) * 0.02
        gate_w = jax.random.normal(ks[5], (N_EXPERTS, D_MODEL), dtype=jnp.float32) * 0.02
        return {'x': x, 'shared_w1': shared_w1, 'shared_w2': shared_w2, 'experts_w1': experts_w1, 'experts_w2': experts_w2, 'gate_w': gate_w}
    _L0_ffn_all = _L0_ffn_setup()
    _L0_ffn_in = {k: v for k, v in _L0_ffn_all.items() if k in ('shared_w1', 'shared_w2', 'experts_w1', 'experts_w2', 'gate_w')}
    del _L0_ffn_all
    return {'x': x, 'ctx_1024': ctx_1024, 'mask_BxS2_bk0': mask_BxS2_bk0, 'L0_xattn_kv_gate': _L0_xattn_in['kv_gate'], 'L0_xattn_gamma_media': _L0_xattn_in['gamma_media'], 'L0_xattn_beta_media': _L0_xattn_in['beta_media'], 'L0_xattn_gamma_lat': _L0_xattn_in['gamma_lat'], 'L0_xattn_beta_lat': _L0_xattn_in['beta_lat'], 'L0_xattn_Wq': _L0_xattn_in['Wq'], 'L0_xattn_Wk': _L0_xattn_in['Wk'], 'L0_xattn_Wv': _L0_xattn_in['Wv'], 'L0_xattn_Wout': _L0_xattn_in['Wout'], 'L0_ffn_shared_w1': _L0_ffn_in['shared_w1'], 'L0_ffn_shared_w2': _L0_ffn_in['shared_w2'], 'L0_ffn_experts_w1': _L0_ffn_in['experts_w1'], 'L0_ffn_experts_w2': _L0_ffn_in['experts_w2'], 'L0_ffn_gate_w': _L0_ffn_in['gate_w']}

def reference(x, ctx_1024, mask_BxS2_bk0, L0_xattn_kv_gate, L0_xattn_gamma_media, L0_xattn_beta_media, L0_xattn_gamma_lat, L0_xattn_beta_lat, L0_xattn_Wq, L0_xattn_Wk, L0_xattn_Wv, L0_xattn_Wout, L0_ffn_shared_w1, L0_ffn_shared_w2, L0_ffn_experts_w1, L0_ffn_experts_w2, L0_ffn_gate_w):
    import jax
    import jax.numpy as jnp

    def _L0_xattn_ref(x, latents, key_padding_mask, kv_gate, gamma_media, beta_media, gamma_lat, beta_lat, Wq, Wk, Wv, Wout):
        import jax, jax.numpy as jnp
        import numpy as np
        HEADS = 8
        DIM_HEAD = 64
        SCALE = DIM_HEAD ** (-0.5)
        LN_EPS = 1e-05
        NEG_INF = -1e+30

        def layernorm(x, gamma, beta):
            mu = jnp.mean(x, axis=-1, keepdims=True)
            var = jnp.var(x, axis=-1, keepdims=True)
            return (x - mu) * jax.lax.rsqrt(var + LN_EPS) * gamma + beta
        b, f, d = x.shape
        n = latents.shape[1]
        x = layernorm(x, gamma_media, beta_media)
        latents = layernorm(latents, gamma_lat, beta_lat)
        kv = jnp.concatenate((x, latents * kv_gate), axis=1)
        q = (latents @ Wq).reshape(b, n, HEADS, DIM_HEAD)
        k = (kv @ Wk).reshape(b, f + n, HEADS, DIM_HEAD)
        v = (kv @ Wv).reshape(b, f + n, HEADS, DIM_HEAD)
        sim = jnp.einsum('bqhd,bkhd->bhqk', q * SCALE, k)
        sim = sim - jax.lax.stop_gradient(jnp.max(sim, axis=-1, keepdims=True))
        valid_feat = ~key_padding_mask
        valid_full = jnp.concatenate((valid_feat, jnp.ones((b, n), dtype=bool)), axis=1)
        sim = jnp.where(valid_full[:, None, None, :], sim, NEG_INF)
        attn = jax.nn.softmax(sim, axis=-1)
        out = jnp.einsum('bhqk,bkhd->bqhd', attn, v).reshape(b, n, HEADS * DIM_HEAD)
        return out @ Wout

    def _L0_attn_ref(x):
        import jax, jax.numpy as jnp
        import numpy as np
        scores = jnp.einsum('bld,bmd->blm', x, x)
        scores = jax.nn.softmax(scores, axis=1)
        return jnp.einsum('blm,bmd->bld', scores, x)

    def _L0_ffn_ref(x, shared_w1, shared_w2, experts_w1, experts_w2, gate_w):
        import jax, jax.numpy as jnp
        import numpy as np
        D_MODEL = 512
        N_EXPERTS = 8
        TOP_K = 2
        HIDDEN = 4 * D_MODEL
        B, S, D = x.shape
        T = B * S
        x_flat = x.reshape(T, D)
        shared = jnp.einsum('td,dh->th', x_flat, shared_w1.T)
        shared = jnp.einsum('th,hd->td', jax.nn.silu(shared), shared_w2.T)
        gate_logits = x_flat @ gate_w.T
        top_k_gates, top_k_idx = jax.lax.top_k(gate_logits, TOP_K)
        top_k_gates = jax.nn.softmax(top_k_gates, axis=1)
        gates = jnp.zeros((T, N_EXPERTS), dtype=x.dtype)
        gates = gates.at[jnp.arange(T)[:, None], top_k_idx].set(top_k_gates)
        h = jnp.einsum('td,ehd->teh', x_flat, experts_w1)
        expert_out = jnp.einsum('teh,edh->ted', jax.nn.silu(h), experts_w2)
        selected = jnp.einsum('ted,te->td', expert_out, gates)
        return (shared + selected).reshape(B, S, D)
    x = x + _L0_xattn_ref(ctx_1024, _layernorm(x, axis=-1), mask_BxS2_bk0, L0_xattn_kv_gate, L0_xattn_gamma_media, L0_xattn_beta_media, L0_xattn_gamma_lat, L0_xattn_beta_lat, L0_xattn_Wq, L0_xattn_Wk, L0_xattn_Wv, L0_xattn_Wout)
    x = x + _L0_attn_ref(_layernorm(x, axis=-1))
    x = x + _L0_ffn_ref(_layernorm(x, axis=-1), L0_ffn_shared_w1, L0_ffn_shared_w2, L0_ffn_experts_w1, L0_ffn_experts_w2, L0_ffn_gate_w)
    return x

_drawn_inputs = setup_inputs


def setup_inputs(seed=0):
    import zlib

    import numpy as np

    out = dict(_drawn_inputs(seed))
    spreads = {'L0_xattn_gamma_media': (1.0, 0.6),
     'L0_xattn_beta_media': (0.0, 1.601),
     'L0_xattn_gamma_lat': (1.0, 0.6),
     'L0_xattn_beta_lat': (0.0, 0.8)}
    factors = {'L0_xattn_Wq': 3.936, 'L0_xattn_Wk': 3.822}
    for name, (base, spread) in spreads.items():
        noise = np.random.default_rng([zlib.crc32(name.encode()), seed]).standard_normal(out[name].shape)
        drawn = base * np.exp(spread * noise) if base else spread * noise
        out[name] = jnp.asarray(drawn.astype(out[name].dtype))
    for name, factor in factors.items():
        out[name] = (out[name] * factor).astype(out[name].dtype)
    return out
```

```python
from contextlib import ExitStack

import concourse.bass as bass
from concourse import mybir

F32 = mybir.dt.float32
F16 = mybir.dt.float16
U8 = mybir.dt.uint8
U32 = mybir.dt.uint32
ALU = mybir.AluOpType
ACT = mybir.ActivationFunctionType
AX = mybir.AxisListType

P = 128
EPS = 1e-5
WEIGHT_SCALE = 256.0
UNSCALE = 1.0 / WEIGHT_SCALE
MASKED = -1e30
LOWEST = -3.0e38


def perceiver_kernel(nc, x, ctx_in, mask, kv_gate, gamma_media, beta_media, gamma_media_cols, gamma_lat, beta_lat,
                     wq, wk_t, wv, wout, w1, w2, gate_w_t, kv_latents, out):
    B, NQ, D = x.shape
    F = ctx_in.shape[1]
    HEADS = 8
    DH = D // HEADS
    DT = D // P
    TOK = B * NQ
    TT = TOK // P
    HQ_TILES = HEADS * NQ // P
    SCALE = float(DH) ** -0.5
    FULL = F // P
    REM = F - FULL * P
    MT = FULL + 1
    KT = MT + 1
    LAT = MT
    KEYS = F + NQ
    CHUNKS = 4
    CH = 416
    LAST = KEYS - (CHUNKS - 1) * CH
    LAST_MEDIA = LAST - NQ
    assert LAST <= 512 and FULL == 12 and DT == 4 and HQ_TILES == 4 and TT == 4

    es = ExitStack()
    first_half = ExitStack()
    with es:
        def keep(name, shape, dt):
            return es.enter_context(nc.sbuf_tensor(name, shape, dt))

        def sb(name, shape, dt):
            return first_half.enter_context(nc.sbuf_tensor(name, shape, dt))

        def sem(name):
            return es.enter_context(nc.semaphore(name))

        xres = keep("residual", [P, TT, D], F32)
        oT = [keep("heads_t_hi", [P, HQ_TILES, TOK], F16), keep("heads_t_lo", [P, HQ_TILES, TOK], F16)]
        ident = keep("ident", [P, P], F32)
        xs = sb("media_f32", [P, KT, D], F32)
        xn = [sb("media_rows_hi", [P, KT, D], F16), sb("media_rows_lo", [P, KT, D], F16)]
        xT = [sb("media_cols_hi", [P, DT, KEYS + 1], F16), sb("media_cols_lo", [P, DT, KEYS + 1], F16)]
        probs = [sb(f"probs{i}", [P, KEYS], F32) for i in range(2)]
        pT = [[sb(f"probs_t{i}_{h}", [P, KT, P], F16) for h in ("hi", "lo")] for i in range(2)]
        qp = [sb("q_keyspace_hi", [P, DT, 512], F16), sb("q_keyspace_lo", [P, DT, 512], F16)]
        wk = [sb("wk_t_hi", [P, DT, D], F16), sb("wk_t_lo", [P, DT, D], F16)]
        wvs = [sb("wv_hi", [P, DT, D], F16), sb("wv_lo", [P, DT, D], F16)]
        qbd = [sb("q_blockdiag_hi", [P, B, HQ_TILES, P], F16), sb("q_blockdiag_lo", [P, B, HQ_TILES, P], F16)]
        qnow = [sb("q_now_hi", [P, HQ_TILES, P], F16), sb("q_now_lo", [P, HQ_TILES, P], F16)]
        mask_u8 = sb("mask_u8", [P, F], U8)
        mask_f = sb("mask_bias", [P, F], F32)
        gm_bc = sb("gamma_media_bc", [P, D], F32)
        bm_bc = sb("beta_media_bc", [P, D], F32)
        gm_col = sb("gamma_media_col", [P, DT], F32)
        gate_c = sb("kv_gate_col", [P, 1], F32)
        usb = sb("u_rows", [P, 2, D], F32)
        uT = [sb("u_cols_hi", [P, DT, P], F16), sb("u_cols_lo", [P, DT, P], F16)]
        stats = sb("stats", [P, MT, 6], F32)
        mv = sb("mean_var", [P, MT, 2], F32)
        rstd = sb("rstd", [P, MT], F32)
        half = sb("minus_half", [P, MT], F32)
        masked = sb("masked_bias", [P, 1], F32)
        bk = sb("beta_wk", [P, DT], F32)
        bkh = [sb("beta_wk_hi", [P, DT], F16), sb("beta_wk_lo", [P, DT], F16)]
        qb_all = sb("q_beta_all", [P, B * HQ_TILES], F32)
        qb_now = sb("q_beta_now", [P, HQ_TILES], F32)
        cmax = sb("chunk_max", [P, 2, 8], F32)
        rmax = sb("row_max", [P, 2, 4], F32)
        rsum = sb("row_sum", [P, 2, 4], F32)
        unorm = sb("u_norm", [P, 4], F32)
        spare = sb("spare", [P, 1 + HQ_TILES * CHUNKS], F32)
        pool_spare = sb("pool_spare", [P, 1], F32)
        psim = [first_half.enter_context(nc.psum_tensor(f"p_sim{i}", [P, 512], F32)) for i in range(CHUNKS)]
        ptp = [first_half.enter_context(nc.psum_tensor(f"p_tp{i}", [P, 512], F32)) for i in range(2)]
        pum = first_half.enter_context(nc.psum_tensor("p_u_media", [P, 512], F32))
        pul = first_half.enter_context(nc.psum_tensor("p_u_latent", [P, 512], F32))

        lat = xT[0][:, :, :].rearrange("p a b -> p (a b)").bitcast(F32)[:, 0:TT * D].rearrange("p (t d) -> p t d", t=TT)
        kvl = xT[1][:, :, :].rearrange("p a b -> p (a b)").bitcast(F32)[:, 0:TT * D].rearrange("p (t d) -> p t d", t=TT)
        wq_f, wk_f, wv_f = xs[:, 0:4, :], xs[:, 4:8, :], xs[:, 8:12, :]
        gl_bc, bl_bc = xs[:, 12, :], xs[:, 13, :]
        latT = [xn[h][:, 0:4, :] for h in range(2)]
        wqs = [xn[h][:, 4:8, :] for h in range(2)]

        s_xin, s_aff, s_wq, s_wk, s_wv = sem("x_loaded"), sem("affine_loaded"), sem("wq_loaded"), sem("wk_loaded"), sem("wv_loaded")
        s_id, s_half, s_zero = sem("ident_ready"), sem("minus_half_ready"), sem("q_blockdiag_zeroed")
        s_st = sem("setup_stats")
        s_rs, s_lr, s_bt, s_qbn = sem("setup_rstd"), sem("latents_step"), sem("beta_step"), sem("q_beta_now_ready")
        s_lat = sem("latents_ready")
        s_kvst = sem("kv_latents_stored")
        s_whi, s_wlo = sem("weights_hi"), sem("weights_lo")
        s_ltp, s_lhi, s_llo = sem("latents_transposed"), sem("latents_t_hi"), sem("latents_t_lo")
        s_qp, s_qhi, s_qlo = sem("q_product"), sem("q_hi"), sem("q_lo")
        s_bk, s_qb, s_qbs = sem("beta_wk_ready"), sem("q_beta_product"), sem("q_beta_ready")
        s_ctx, s_mk = sem("ctx_loaded"), sem("mask_loaded")
        s_mc, s_mf = sem("mask_as_float"), sem("mask_ready")
        s_bs, s_ve, s_rd = sem("media_stats"), sem("media_var"), sem("media_rstd")
        s_norm = sem("media_normalised")
        s_nh, s_nl = sem("media_rows_hi_ready"), sem("media_rows_lo_ready")
        s_qn = sem("q_now_ready")
        s_sim, s_sfree = sem("sim_ready"), sem("sim_free")
        s_rm, s_exp = sem("row_max_step"), sem("probs_ready")
        s_tp, s_thi, s_tfree = sem("tp_ready"), sem("tp_hi"), sem("tp_free")
        s_xp, s_xhi, s_xfree = sem("prep_ready"), sem("prep_hi"), sem("prep_free")
        s_pv, s_u = sem("pv_ready"), sem("u_step")

        AFTER = [{3: [("P", 0, 2)], 7: [("P", 0, 3)]},
                 {1: [("U", 0)], 3: [("P", 1, 2)], 7: [("P", 1, 3)], 10: [("V", 0)]},
                 {1: [("U", 1)], 3: [("P", 2, 2)], 5: [("x", 0)], 6: [("x", 1)], 7: [("P", 2, 3)], 8: [("x", 2)],
                  9: [("x", 3)], 10: [("V", 1), ("x", 4)], 11: [("x", 5)], 12: [("x", 6)],
                  13: [("P", 3, 0), ("P", 3, 1), ("x", 7)]},
                 {0: [("x", 8)], 1: [("x", 9)], 2: [("x", 10)], 3: [("P", 3, 2)], 4: [("U", 2)], 5: [("x", 11)],
                  6: [("x", 12)], 7: [("P", 3, 3)], 8: [("x", 13)], 9: [("q", 0)], 10: [("V", 2), ("q", 1)],
                  11: [("q", 2)], 12: [("q", 3)]}]
        ROUNDS = 24
        PREP = [("x", i) for i in range(14)] + [("q", i) for i in range(4)]
        NPREP = len(PREP)

        def kept(rounds, last):
            return [r for r in rounds if not (last and r[0] in "xq")]

        def cells(t, last, tiles=range(KT)):
            return kept([r for k in tiles for r in AFTER[t].get(k, [])], last)

        def rows(k):
            return P if k < FULL else (REM if k == FULL else NQ)

        block = first_half.enter_context(nc.Block())

        @block.sync
        def _(sp):
            sp.dma_start(xres[:], x.rearrange("b n d -> (b n) d").rearrange("(t p) d -> p t d", p=P)).then_inc(s_xin, 16)
            sp.dma_start(wq_f, wq.rearrange("(t p) n -> p t n", p=P)).then_inc(s_wq, 16)
            sp.dma_start(wk_f, wk_t.rearrange("(t p) n -> p t n", p=P)).then_inc(s_wk, 16)
            sp.dma_start(wv_f, wv.rearrange("(t p) n -> p t n", p=P)).then_inc(s_wv, 16)
            sp.wait_ge(s_lat, 2 * TT)
            sp.dma_start(kv_latents.rearrange("(t p) d -> p t d", p=P), kvl).then_inc(s_kvst, 16)
            sp.wait_ge(s_kvst, 16)

            def load_batch(b, first):
                if first:
                    sp.wait_ge(s_whi, 3)
                    sp.wait_ge(s_wlo, 3)
                    sp.wait_ge(s_bk, 1)
                else:
                    sp.wait_ge(s_nh, KT * b)
                    sp.wait_ge(s_nl, KT * b)
                    sp.wait_ge(s_mf, b)
                bs = bass.ds(b, 1) if not isinstance(b, int) else slice(b, b + 1)
                sp.dma_start(xs[:, 0:FULL, :], ctx_in[bs, 0:FULL * P, :].rearrange("o (t p) d -> p (o t) d", p=P)).then_inc(s_ctx, 16)
                sp.dma_start(xs[0:REM, FULL, :], ctx_in[bs, FULL * P:F, :].rearrange("o p d -> (o p) d")).then_inc(s_ctx, 16)
                sp.dma_start(xs[0:NQ, LAT, :], kv_latents.rearrange("(b n) d -> b n d", n=NQ)[bs, :, :].rearrange("o p d -> (o p) d")).then_inc(s_ctx, 16)
                sp.dma_start(mask_u8[:, :], mask[bs, :].broadcast_to((P, F))).then_inc(s_mk, 16)

            load_batch(0, True)
            with sp.Fori(1, B) as b:
                load_batch(b, False)

        @block.gpsimd
        def _(pool):
            pool.dma_start(gl_bc, gamma_lat.broadcast_to((P, D))).then_inc(s_aff, 16)
            pool.dma_start(bl_bc, beta_lat.broadcast_to((P, D))).then_inc(s_aff, 16)
            pool.dma_start(gm_bc[:], gamma_media.broadcast_to((P, D))).then_inc(s_aff, 16)
            pool.dma_start(bm_bc[:], beta_media.broadcast_to((P, D))).then_inc(s_aff, 16)
            pool.dma_start(gm_col[:], gamma_media_cols).then_inc(s_aff, 16)
            pool.dma_start(gate_c[:], kv_gate.broadcast_to((P, 1))).then_inc(s_aff, 16)
            pool.memset(ident[:], 0.0).then_inc(s_id, 1)
            pool.memset(masked[:], MASKED).then_inc(s_half, 1)
            pool.memset(half[:], -0.5).then_inc(s_half, 1)
            pool.wait_ge(s_id, 1)
            pool.affine_select(out=ident[:], in_=ident[:], compare_op=ALU.not_equal, fill=1.0, base=0,
                               pattern=[[-1, P]], channel_multiplier=1).then_inc(s_id, 1)
            pool.wait_ge(s_half, 2)
            for n in range(2):
                pool.wait_ge(s_st, 3 * (n + 1))
                pool.tensor_tensor(rstd[:, 0:TT], mv[:, 0:TT, 1], half[:, 0:TT], ALU.pow).then_inc(s_rs, 1)

            def media_rstd(n):
                pool.wait_ge(s_ve, n)
                pool.tensor_tensor(rstd[:], mv[:, :, 1], half[:], ALU.pow).then_inc(s_rd, 1)

            def mask_bias(b1):
                pool.wait_ge(s_mk, b1 * 16)
                pool.tensor_tensor(pool_spare[:], masked[:], masked[:], ALU.add)
                pool.tensor_copy(mask_f[:], mask_u8[:]).then_inc(s_mc, 1)
                pool.wait_ge(s_mc, b1)
                pool.tensor_tensor(mask_f[:], mask_f[:], masked[:, 0:1].broadcast_to((P, F)), ALU.mult).then_inc(s_mf, 1)

            media_rstd(1)
            mask_bias(1)
            with pool.Fori(1, B) as b:
                media_rstd(b + 1)
                pool.wait_ge(s_sfree, CHUNKS * HQ_TILES * b)
                mask_bias(b + 1)

        @block.scalar
        def _(act):
            def split_hi(out_, in_, scale=1.0):
                return act.activation(out_, in_, ACT.Copy, scale=scale)

            act.wait_ge(s_wq, 16)
            split_hi(wqs[0], wq_f, WEIGHT_SCALE).then_inc(s_whi, 1)
            act.wait_ge(s_wk, 16)
            split_hi(wk[0][:], wk_f, WEIGHT_SCALE).then_inc(s_whi, 1)
            act.wait_ge(s_wv, 16)
            split_hi(wvs[0][:], wv_f, WEIGHT_SCALE).then_inc(s_whi, 1)
            for dt in range(DT):
                act.wait_ge(s_ltp, dt + 1)
                split_hi(latT[0][:, dt, :], psim[dt][:]).then_inc(s_lhi, 1)
            act.wait_ge(s_zero, 1)
            for t in range(HQ_TILES):
                act.wait_ge(s_qp, t + 1)
                for i in range(2):
                    src = [*ptp, pum, pul][t][64 * i:64 * i + 64, :].rearrange("p (b n) -> p b n", n=NQ)
                    last = split_hi(qbd[0][64 * i:64 * i + 64, :, t, 64 * i:64 * i + 64], src, UNSCALE)
                last.then_inc(s_qhi, 1)

            rnd = [0]

            def take(kind, b):
                if kind[0] in "xq":
                    r = PREP.index(kind)
                    p, done = psim[r % 4], s_xhi
                    act.wait_ge(s_xp, NPREP * b + r + 1)
                else:
                    r = rnd[0]
                    rnd[0] += 1
                    p, done = ptp[r % 2], s_thi
                    act.wait_ge(s_tp, ROUNDS * b + r + 1)
                if kind[0] == "P":
                    dst = pT[kind[1] % 2][0]
                    if kind[2] < 3:
                        split_hi(dst[:, 4 * kind[2]:4 * kind[2] + 4, :], p[:].rearrange("p (k q) -> p k q", q=P)).then_inc(done, 1)
                    else:
                        split_hi(dst[0:REM, FULL, :], p[0:REM, 0:P])
                        split_hi(dst[0:NQ, LAT, :], p[0:NQ, P:2 * P]).then_inc(done, 1)
                elif kind[0] == "x":
                    i = kind[1]
                    if i < 12:
                        act.activation(xT[0][:, i % 4, (i // 4) * 512:(i // 4) * 512 + 512], p[:], ACT.Copy,
                                       scale=gm_col[:, i % 4:i % 4 + 1]).then_inc(done, 1)
                    elif i == 12:
                        for dt in range(DT):
                            last = act.activation(xT[0][:, dt, FULL * P:F], p[:, dt * REM:(dt + 1) * REM], ACT.Copy,
                                                  scale=gm_col[:, dt:dt + 1])
                        last.then_inc(done, 1)
                    else:
                        split_hi(xT[0][:, :, F:KEYS], p[:].rearrange("p (t q) -> p t q", t=DT)[:, :, 0:NQ]).then_inc(done, 1)
                elif kind[0] == "q":
                    split_hi(qp[0][:, kind[1], :], p[:], UNSCALE).then_inc(done, 1)
                elif kind[0] == "U":
                    split_hi(uT[0][:], p[:].rearrange("p (t q) -> p t q", t=DT)).then_inc(done, 1)
                else:
                    for i in range(2):
                        s = slice(64 * i, 64 * i + 64)
                        last = split_hi(oT[0][s, kind[1], bass.ds(b * NQ, NQ)], p[s, 64 * i:64 * i + 64], UNSCALE)
                    last.then_inc(done, 1)

            def exponentials(t, b):
                act.wait_ge(s_rm, 4 * (HQ_TILES * b + t) + 4)
                pr = probs[t % 2]
                act.activation(pr[:, 0:F], pr[:, 0:F], ACT.Exp, bias=rmax[:, t % 2, 3:4],
                               accum_out=rsum[:, t % 2, 0:1])
                act.activation(pr[:, F:KEYS], pr[:, F:KEYS], ACT.Exp, bias=rmax[:, t % 2, 2:3],
                               accum_out=rsum[:, t % 2, 1:2]).then_inc(s_exp, 1)

            for r in PREP:
                take(r, 0)

            def row_high(b, first):
                act.wait_ge(s_norm, MT * (b + 1))
                act.wait_ge(s_ctx, 48 * (b + 1))
                if not first:
                    act.wait_ge(s_pv, HQ_TILES * b)
                for k in range(KT):
                    n = NQ if k == LAT else P
                    split_hi(xn[0][0:n, k, :], xs[0:n, k, :]).then_inc(s_nh, 1)

            def batch(b, first, last):
                row_high(b, first)
                if not first:
                    rnd[0] = ROUNDS - 2
                    take(("U", 3), b - 1)
                exponentials(0, b)
                if not first:
                    take(("V", 3), b - 1)
                rnd[0] = 0
                take(("P", 0, 0), b)
                take(("P", 0, 1), b)
                exponentials(1, b)
                for r in cells(0, last):
                    take(r, b)
                for t in (1, 2):
                    take(("P", t, 0), b)
                    take(("P", t, 1), b)
                    exponentials(t + 1, b)
                    for r in cells(t, last):
                        take(r, b + 1 if r[0] in "xq" else b)
                for r in cells(3, last):
                    take(r, b + 1 if r[0] in "xq" else b)

            batch(0, True, False)
            with act.Fori(1, B - 1) as b:
                batch(b, False, False)
            batch(B - 1, False, True)
            take(("U", 3), B - 1)
            take(("V", 3), B - 1)

        @block.vector
        def _(dve):
            def split_lo(out_, in_, hi, scale=1.0):
                return dve.scalar_tensor_tensor(out_, in_, scale, hi, ALU.mult, ALU.subtract)

            dve.memset(qbd[0][:], 0.0)
            dve.memset(qbd[1][:], 0.0).then_inc(s_zero, 1)
            dve.wait_ge(s_xin, 16)
            n = 0
            for rep, src in ((0, xres), (1, lat)):
                for t in range(TT):
                    last = dve.bn_stats(stats[:, t, :], src[:, t, :])
                last.then_inc(s_st, 1)
                dve.wait_ge(s_st, 3 * rep + 1)
                if rep:
                    dve.wait_ge(s_rs, 1)
                for t in range(TT):
                    last = dve.bn_aggr(mv[:, t, :], stats[:, t, :])
                last.then_inc(s_st, 1)
                dve.wait_ge(s_st, 3 * rep + 2)
                dve.tensor_scalar(mv[:, 0:TT, 1], mv[:, 0:TT, 1], EPS, None, ALU.add).then_inc(s_st, 1)
                dve.wait_ge(s_rs, rep + 1)
                for t in range(TT):
                    last = dve.tensor_scalar(lat[:, t, :], src[:, t, :], mv[:, t, 0:1], rstd[:, t:t + 1], ALU.subtract, ALU.mult)
                last.then_inc(s_lr, 1)
                dve.wait_ge(s_lr, rep + 1)
            dve.wait_ge(s_aff, 96)
            for t in range(TT):
                last = dve.tensor_tensor(lat[:, t, :], lat[:, t, :], gl_bc, ALU.mult)
            last.then_inc(s_lr, 1)
            dve.wait_ge(s_lr, 3)
            for t in range(TT):
                dve.tensor_tensor(lat[:, t, :], lat[:, t, :], bl_bc, ALU.add).then_inc(s_lat, 1)
            dve.wait_ge(s_lat, TT)
            for t in range(TT):
                dve.tensor_scalar(kvl[:, t, :], lat[:, t, :], gate_c[:, 0:1], None, ALU.mult).then_inc(s_lat, 1)
            for n, (w, f) in enumerate(((wqs, wq_f), (wk, wk_f), (wvs, wv_f))):
                dve.wait_ge(s_whi, n + 1)
                for dt in range(DT):
                    last = split_lo(w[1][:, dt, :], f[:, dt, :], w[0][:, dt, :], WEIGHT_SCALE)
                last.then_inc(s_wlo, 1)
            for t in range(DT):
                last = dve.tensor_tensor_reduce(usb[:, 0, :] if t % 2 == 0 else usb[:, 1, :], wk_f[:, t, :], bm_bc[:], 1.0, 0.0, ALU.mult, ALU.add, bk[:, t:t + 1])
                last.then_inc(s_bt, 1)
                dve.wait_ge(s_bt, t + 1)
            dve.tensor_copy(bkh[0][:], bk[:]).then_inc(s_bt, 1)
            dve.wait_ge(s_bt, DT + 1)
            dve.memset(xs[:, FULL:KT, :], 0.0).then_inc(s_bt, 1)
            dve.tensor_tensor(bkh[1][:], bk[:], bkh[0][:], ALU.subtract).then_inc(s_bk, 1)
            for dt in range(DT):
                dve.wait_ge(s_lhi, dt + 1)
                split_lo(latT[1][:, dt, :], psim[dt][:], latT[0][:, dt, :]).then_inc(s_llo, 1)
            for t in range(HQ_TILES):
                dve.wait_ge(s_qhi, t + 1)
                for i in range(2):
                    s = slice(64 * i, 64 * i + 64)
                    src = [*ptp, pum, pul][t][s, :].rearrange("p (b n) -> p b n", n=NQ)
                    last = split_lo(qbd[1][s, :, t, s], src, qbd[0][s, :, t, s], UNSCALE)
                last.then_inc(s_qlo, 1)
            dve.wait_ge(s_qlo, HQ_TILES)
            dve.wait_ge(s_qb, 1)
            dve.tensor_scalar(qb_all[:], psim[0][:, 0:B * HQ_TILES], SCALE, None, ALU.mult).then_inc(s_qbs, 1)
            dve.wait_ge(s_qbs, 1)

            def media_stats(b1, tiles):
                if 0 in tiles:
                    dve.wait_ge(s_ctx, 48 * b1)
                for k in tiles:
                    last = dve.bn_stats(stats[:, k, :], xs[:, k, :])
                if MT - 1 not in tiles:
                    return
                last.then_inc(s_bs, 1)
                dve.wait_ge(s_bs, 2 * b1 - 1)
                dve.tensor_copy(spare[:, 0:1], stats[:, MT - 1, 0:1])
                for k in range(MT):
                    last = dve.bn_aggr(mv[:, k, :], stats[:, k, :])
                last.then_inc(s_bs, 1)
                dve.wait_ge(s_bs, 2 * b1)
                dve.tensor_scalar(mv[:, :, 1], mv[:, :, 1], EPS, None, ALU.add).then_inc(s_ve, 1)

            def queries(b):
                for h in range(2):
                    last = dve.tensor_copy(qnow[h][:], qbd[h][:, bass.ds(b, 1), :, :].rearrange("p o t q -> p (o t) q"))
                last.then_inc(s_qn, 1)

            rnd = [0]

            def take(kind, b):
                if kind[0] in "xq":
                    r = PREP.index(kind)
                    p, done = psim[r % 4], s_xfree
                    dve.wait_ge(s_xhi, NPREP * b + r + 1)
                else:
                    r = rnd[0]
                    rnd[0] += 1
                    p, done = ptp[r % 2], s_tfree
                    dve.wait_ge(s_thi, ROUNDS * b + r + 1)
                if kind[0] == "P":
                    hi, lo = pT[kind[1] % 2]
                    if kind[2] < 3:
                        s = slice(4 * kind[2], 4 * kind[2] + 4)
                        split_lo(lo[:, s, :], p[:].rearrange("p (k q) -> p k q", q=P), hi[:, s, :]).then_inc(done, 1)
                    else:
                        split_lo(lo[0:REM, FULL, :], p[0:REM, 0:P], hi[0:REM, FULL, :])
                        split_lo(lo[0:NQ, LAT, :], p[0:NQ, P:2 * P], hi[0:NQ, LAT, :]).then_inc(done, 1)
                elif kind[0] == "x":
                    i = kind[1]
                    if i < 12:
                        s = slice((i // 4) * 512, (i // 4) * 512 + 512)
                        split_lo(xT[1][:, i % 4, s], p[:], xT[0][:, i % 4, s], gm_col[:, i % 4:i % 4 + 1]).then_inc(done, 1)
                    elif i == 12:
                        for dt in range(DT):
                            last = split_lo(xT[1][:, dt, FULL * P:F], p[:, dt * REM:(dt + 1) * REM],
                                            xT[0][:, dt, FULL * P:F], gm_col[:, dt:dt + 1])
                        last.then_inc(done, 1)
                    else:
                        split_lo(xT[1][:, :, F:KEYS], p[:].rearrange("p (t q) -> p t q", t=DT)[:, :, 0:NQ],
                                 xT[0][:, :, F:KEYS]).then_inc(done, 1)
                elif kind[0] == "q":
                    split_lo(qp[1][:, kind[1], :], p[:], qp[0][:, kind[1], :], UNSCALE).then_inc(done, 1)
                elif kind[0] == "U":
                    split_lo(uT[1][:], p[:].rearrange("p (t q) -> p t q", t=DT), uT[0][:]).then_inc(done, 1)
                else:
                    for i in range(2):
                        s = slice(64 * i, 64 * i + 64)
                        o = bass.ds(b * NQ, NQ)
                        last = split_lo(oT[1][s, kind[1], o], p[s, 64 * i:64 * i + 64], oT[0][s, kind[1], o], UNSCALE)
                    last.then_inc(done, 1)

            def chunk_max(t, c, b):
                dve.wait_ge(s_sim, CHUNKS * (HQ_TILES * b + t) + c + 1)
                dve.tensor_copy(spare[:, 1 + CHUNKS * t + c:2 + CHUNKS * t + c], psim[c][:, 0:1])
                m = LAST_MEDIA if c == CHUNKS - 1 else CH
                lo = c * CH
                ins = dve.tensor_tensor_reduce(probs[t % 2][:, lo:lo + m], psim[c][:, 0:m], mask_f[:, lo:lo + m], SCALE, LOWEST,
                                               ALU.add, ALU.max, cmax[:, t % 2, c:c + 1])
                if c == CHUNKS - 1:
                    ins = dve.tensor_scalar(probs[t % 2][:, F:KEYS], psim[c][:, m:m + NQ], SCALE, LOWEST, ALU.mult, ALU.max,
                                            accum_out=cmax[:, t % 2, 4:5])
                ins.then_inc(s_sfree, 1)

            def row_max(t, b):
                n = 4 * (HQ_TILES * b + t)
                c, m = cmax[:, t % 2, :], rmax[:, t % 2, :]
                dve.wait_ge(s_sfree, CHUNKS * (HQ_TILES * b + t) + CHUNKS)
                dve.tensor_reduce(m[:, 0:1], c[:, 0:4], AX.X, ALU.max).then_inc(s_rm, 1)
                dve.wait_ge(s_rm, n + 1)
                dve.scalar_tensor_tensor(m[:, 1:2], m[:, 0:1], qb_now[:, t:t + 1], c[:, 4:5], ALU.add, ALU.max).then_inc(s_rm, 1)
                dve.wait_ge(s_rm, n + 2)
                dve.tensor_scalar(m[:, 2:3], m[:, 1:2], -1.0, None, ALU.mult).then_inc(s_rm, 1)
                dve.tensor_tensor(m[:, 3:4], qb_now[:, t:t + 1], m[:, 1:2], ALU.subtract).then_inc(s_rm, 1)

            def attended(t, b):
                n = 6 * (HQ_TILES * b + t)
                s = rsum[:, t % 2, :]
                dve.tensor_tensor(unorm[:, 0:1], s[:, 0:1], s[:, 1:2], ALU.add).then_inc(s_u, 1)
                dve.wait_ge(s_u, n + 1)
                dve.reciprocal(unorm[:, 1:2], unorm[:, 0:1]).then_inc(s_u, 1)
                dve.wait_ge(s_u, n + 2)
                dve.tensor_tensor(unorm[:, 2:3], unorm[:, 1:2], s[:, 0:1], ALU.mult).then_inc(s_u, 1)
                dve.wait_ge(s_pv, HQ_TILES * b + t + 1)
                dve.scalar_tensor_tensor(usb[:, 0, :], pum[:], unorm[:, 1:2], gm_bc[:], ALU.mult, ALU.mult).then_inc(s_u, 1)
                dve.wait_ge(s_u, n + 4)
                dve.scalar_tensor_tensor(usb[:, 1, :], bm_bc[:], unorm[:, 2:3], usb[:, 0, :], ALU.mult, ALU.add).then_inc(s_u, 1)
                dve.wait_ge(s_u, n + 5)
                dve.scalar_tensor_tensor(usb[:, 0, :], pul[:], unorm[:, 1:2], usb[:, 1, :], ALU.mult, ALU.add).then_inc(s_u, 1)

            def row_low(tiles, b):
                for k in tiles:
                    n = NQ if k == LAT else P
                    dve.wait_ge(s_nh, KT * b + k + 1)
                    dve.tensor_tensor(xn[1][0:n, k, :], xs[0:n, k, :], xn[0][0:n, k, :], ALU.subtract).then_inc(s_nl, 1)

            def normalise(tiles, n):
                dve.wait_ge(s_rd, n)
                for k in tiles:
                    dve.tensor_scalar(xs[:, k, :], xs[:, k, :], mv[:, k, 0:1], rstd[:, k:k + 1],
                                      ALU.subtract, ALU.mult).then_inc(s_norm, 1)

            media_stats(1, range(MT))
            queries(0)
            normalise(range(MT), 1)
            for r in PREP:
                take(r, 0)

            def batch(b, first, last):
                if not first:
                    attended(3, b - 1)
                dve.tensor_copy(qb_now[:], qb_all[:, bass.ds(b * HQ_TILES, HQ_TILES)]).then_inc(s_qbn, 1)
                dve.wait_ge(s_mf, b + 1)
                for c in range(CHUNKS):
                    chunk_max(0, c, b)
                    if c < 3:
                        row_low(range(3 * c, 3 * c + 3), b)
                dve.wait_ge(s_qbn, b + 1)
                row_max(0, b)
                row_low(range(9, KT), b)
                if not first:
                    rnd[0] = ROUNDS - 2
                    take(("U", 3), b - 1)
                chunk_max(1, 0, b)
                chunk_max(1, 1, b)
                if not first:
                    take(("V", 3), b - 1)
                rnd[0] = 0
                chunk_max(1, 2, b)
                take(("P", 0, 0), b)
                chunk_max(1, 3, b)
                take(("P", 0, 1), b)
                row_max(1, b)
                for r in cells(0, last):
                    take(r, b)
                attended(0, b)
                for c in range(CHUNKS):
                    chunk_max(2, c, b)
                    if c > 1:
                        take(("P", 1, c - 2), b)
                row_max(2, b)
                for i, r in enumerate(cells(1, last)):
                    take(r, b)
                    if not last:
                        media_stats(b + 2, range(4 * i, min(4 * i + 4, MT)))
                attended(1, b)
                for c in range(CHUNKS):
                    chunk_max(3, c, b)
                    if not last and c < 3:
                        normalise(range(c * 5, min(c * 5 + 5, MT)), b + 2)
                    if c > 1:
                        take(("P", 2, c - 2), b)
                row_max(3, b)
                if not last:
                    queries(b + 1)
                for r in cells(2, last):
                    take(r, b + 1 if r[0] in "xq" else b)
                attended(2, b)
                for r in cells(3, last):
                    take(r, b + 1 if r[0] in "xq" else b)

            batch(0, True, False)
            with dve.Fori(1, B - 1) as b:
                batch(b, False, False)
            batch(B - 1, False, True)
            attended(3, B - 1)
            take(("U", 3), B - 1)
            take(("V", 3), B - 1)

        @block.tensor
        def _(pe):
            def product(out_, lhs, rhs, first, last):
                pe.matmul(out_, lhs[0], rhs[0], start=first, stop=False)
                pe.matmul(out_, lhs[0], rhs[1], start=False, stop=False)
                return pe.matmul(out_, lhs[1], rhs[0], start=False, stop=last)

            pe.wait_ge(s_id, 2)
            pe.wait_ge(s_lat, TT)
            for dt in range(DT):
                for t in range(TT):
                    last = pe.transpose(psim[dt][:, t * P:(t + 1) * P], lat[:, t, dt * P:(dt + 1) * P], ident[:])
                last.then_inc(s_ltp, 1)
            pe.wait_ge(s_wlo, 1)
            pe.wait_ge(s_llo, DT)
            for t in range(HQ_TILES):
                for dt in range(DT):
                    last = product([*ptp, pum, pul][t][:], [w[:, dt, t * P:(t + 1) * P] for w in wqs],
                                   [l[:, dt, :] for l in latT], dt == 0, dt == DT - 1)
                last.then_inc(s_qp, 1)
            pe.wait_ge(s_bk, 1)
            pe.wait_ge(s_qlo, HQ_TILES)
            for b in range(B):
                for t in range(HQ_TILES):
                    n = b * HQ_TILES + t
                    last = product(psim[0][:, n:n + 1], [q[:, b, t, :] for q in qbd], [v[:, t:t + 1] for v in bkh], True, True)
            last.then_inc(s_qb, 1)

            rnd = [0]

            u_round = {}

            def give(kind, b):
                if kind[0] in "xq":
                    r = PREP.index(kind)
                    p, done = psim[r % 4], s_xp
                    if r >= 4:
                        pe.wait_ge(s_xfree, NPREP * b + r - 3)
                    elif not (isinstance(b, int) and b == 0):
                        pe.wait_ge(s_sfree, CHUNKS * (HQ_TILES * b - 1) + r + 1)
                else:
                    r = rnd[0]
                    rnd[0] += 1
                    p, done = ptp[r % 2], s_tp
                    if not (isinstance(b, int) and b == 0 and r < 2):
                        pe.wait_ge(s_tfree, ROUNDS * b + r - 1)
                if kind[0] == "P":
                    t, g = kind[1], kind[2]
                    if g == 0:
                        pe.wait_ge(s_exp, HQ_TILES * b + t + 1)
                    tiles = range(4 * g, 4 * g + 4) if g < 3 else (FULL, LAT)
                    for i, k in enumerate(tiles):
                        n = rows(k)
                        c = k * P if k < LAT else F
                        last = pe.transpose(p[0:n, i * P:(i + 1) * P], probs[t % 2][:, c:c + n], ident[:])
                elif kind[0] == "x":
                    i = kind[1]
                    if i < 12:
                        if i % 4 == 0:
                            pe.wait_ge(s_norm, MT * b + 4 * (i // 4) + 4)
                        for j in range(4):
                            last = pe.transpose(p[:, j * P:(j + 1) * P], xs[:, (i // 4) * 4 + j, (i % 4) * P:(i % 4 + 1) * P], ident[:])
                    else:
                        k, n = (FULL, REM) if i == 12 else (LAT, P)
                        pe.wait_ge(s_norm, MT * (b + 1)) if i == 12 else pe.wait_ge(s_ctx, 48 * (b + 1))
                        for dt in range(DT):
                            last = pe.transpose(p[:, dt * n:(dt + 1) * n], xs[0:n, k, dt * P:(dt + 1) * P], ident[0:n, 0:n])
                elif kind[0] == "q":
                    dt = kind[1]
                    pe.wait_ge(s_qn, b + 1)
                    for t in range(HQ_TILES):
                        last = product(p[:, t * P:(t + 1) * P], [w[:, t, dt * P:(dt + 1) * P] for w in wk], [q[:, t, :] for q in qnow], True, True)
                elif kind[0] == "U":
                    u_round[kind[1]] = r
                    pe.wait_ge(s_u, 6 * (HQ_TILES * b + kind[1]) + 6)
                    for dt in range(DT):
                        last = pe.transpose(p[:, dt * P:(dt + 1) * P], usb[:, 0, dt * P:(dt + 1) * P], ident[:])
                else:
                    t = kind[1]
                    pe.wait_ge(s_tfree, ROUNDS * b + u_round[t] + 1)
                    for dt in range(DT):
                        last = product(p[:, 0:P], [w[:, dt, t * P:(t + 1) * P] for w in wvs], [u[:, dt, :] for u in uT], dt == 0, dt == DT - 1)
                last.then_inc(done, 1)
                return r

            def scores(t, c, b):
                if t > 0:
                    pe.wait_ge(s_sfree, CHUNKS * (HQ_TILES * b + t - 1) + c + 1)
                n = LAST if c == CHUNKS - 1 else CH
                for dt in range(DT):
                    last = product(psim[c][:, 0:n], [q[:, dt, t * P:(t + 1) * P] for q in qp],
                                   [v[:, dt, c * CH:c * CH + n] for v in xT], dt == 0, dt == DT - 1)
                last.then_inc(s_sim, 1)

            def attend(t, k, b):
                if k == 0:
                    if not (isinstance(b, int) and b == 0 and t == 0):
                        pe.wait_ge(s_u, 6 * (HQ_TILES * b + t) - 2)
                    if t == 0:
                        pe.wait_ge(s_nl, KT * (b + 1))
                if k == LAT and not (isinstance(b, int) and b == 0 and t == 0):
                    pe.wait_ge(s_u, 6 * (HQ_TILES * b + t))
                if k % 4 == 0:
                    pe.wait_ge(s_tfree, ROUNDS * b + p_rounds[t][k // 4] + 1)
                n = rows(k)
                o = pul if k == LAT else pum
                last = product(o[:], [q[0:n, k, :] for q in pT[t % 2]], [v[0:n, k, :] for v in xn],
                               k in (0, LAT), k in (FULL, LAT))
                if k == LAT:
                    last.then_inc(s_pv, 1)

            pe.wait_ge(s_wlo, 3)
            pe.wait_ge(s_qbs, 1)
            for r in PREP:
                give(r, 0)

            def batch(b, first, last):
                def attend_all(t):
                    for k in range(KT):
                        attend(t, k, b)
                        for r in cells(t, last, [k]):
                            n = give(r, b + 1 if r[0] in "xq" else b)
                            if r[0] == "P":
                                p_rounds[r[1]].append(n)

                pe.wait_ge(s_xfree, NPREP * (b + 1))
                for c in range(CHUNKS):
                    scores(0, c, b)
                if not first:
                    rnd[0] = ROUNDS - 2
                    give(("U", 3), b - 1)
                for c in range(CHUNKS):
                    scores(1, c, b)
                    if c == 1:
                        if not first:
                            give(("V", 3), b - 1)
                        rnd[0] = 0
                        for q in p_rounds:
                            q.clear()
                    if c > 1:
                        p_rounds[0].append(give(("P", 0, c - 2), b))
                attend_all(0)
                for t in (1, 2):
                    for c in range(CHUNKS):
                        scores(t + 1, c, b)
                        if c > 1:
                            p_rounds[t].append(give(("P", t, c - 2), b))
                    attend_all(t)
                attend_all(3)

            p_rounds = [[], [], [], []]
            batch(0, True, False)
            with pe.Fori(1, B - 1) as b:
                batch(b, False, False)
            batch(B - 1, False, True)
            give(("U", 3), B - 1)
            give(("V", 3), B - 1)

        first_half.close()
        if w1 is None:
            blk2 = es.enter_context(nc.Block())
            s_dump = sem("dump")

            @blk2.sync
            def _(sp):
                for h in range(2):
                    sp.dma_start(out[h], oT[h][:]).then_inc(s_dump, 16)
                sp.wait_ge(s_dump, 32)
            return
        second_half(nc, es, xres, oT, ident, wout, w1, w2, gate_w_t, out)


def second_half(nc, es, xres, oT, ident, wout, w1, w2, gate_w_t, out):
    TT, D = xres.shape[1], xres.shape[2]
    DT = D // P
    TOK = TT * P
    NQ = P // 2
    NSETS, NJ, _, _, HC = w1.shape
    HT = HC // P
    E = gate_w_t.shape[2]

    def sb(name, shape, dt):
        return es.enter_context(nc.sbuf_tensor(name, shape, dt))

    def sem(name):
        return es.enter_context(nc.semaphore(name))

    wo_f = sb("wout_f32", [P, DT, D], F32)
    wo = [sb("wout_hi", [P, DT, D], F16), sb("wout_lo", [P, DT, D], F16)]
    gw_f = sb("gate_w_f32", [P, DT, E], F32)
    gw = [sb("gate_w_hi", [P, DT, E], F16), sb("gate_w_lo", [P, DT, E], F16)]
    x1 = sb("x_after_media", [P, TT, D], F32)
    x2n = sb("x_self_norm", [P, TT, D], F32)
    x2T = sb("x_self_norm_t", [P, TT, DT, P], F32)
    acc = sb("x_after_self", [P, TT, D], F32)
    x3n = sb("x_ffn_norm", [P, TT, D], F32)
    x3T = [sb("x_ffn_t_hi", [P, DT, TOK], F16), sb("x_ffn_t_lo", [P, DT, TOK], F16)]
    stats = sb("stats2", [P, TT, 6], F32)
    mv = sb("mean_var2", [P, TT, 2], F32)
    rstd = sb("rstd2", [P, TT], F32)
    half = sb("minus_half2", [P, TT], F32)
    pbd = sb("self_probs", [P, TT, P], F32)
    smax = sb("self_max", [P, TT], F32)
    ssum = sb("self_sum", [P, TT], F32)
    srec = sb("self_rec", [P, TT], F32)
    iota8 = sb("iota8", [P, E], F32)
    logits = sb("gate_logits", [P, TT, E], F32)
    top = sb("top_values", [P, TT, 8], F32)
    topi = sb("top_index", [P, TT, 8], U32)
    topf = sb("top_index_f", [P, TT, 2], F32)
    gate = sb("gate_step", [P, TT, 4], F32)
    gates = sb("gates", [P, TT, NSETS], F32)
    g1hot = sb("gate_second", [P, TT, E], F32)
    wst = [[sb(f"w{k + 1}_f32_{i}", [P, 4, HC], F32) for i in range(2)] for k in range(2)]
    wsp = [[[sb(f"w{k + 1}_{h}_{i}", [P, 4, HC], F16) for h in ("hi", "lo")] for i in range(2)] for k in range(2)]
    hf = sb("hidden_f32", [P, 2, TOK], F32)
    hT = [[sb(f"hidden_{h}_{i}", [P, HT, TOK], F16) for h in ("hi", "lo")] for i in range(2)]
    pb = [es.enter_context(nc.psum_tensor(f"p_bank{i}", [P, 512], F32)) for i in range(8)]

    s_wo, s_gw = sem("wout_loaded"), sem("gate_w_loaded")
    s_woh, s_wol = sem("wout_hi_ready"), sem("wout_lo_ready")
    s_y, s_x1 = sem("out_projected"), sem("x1_ready")
    s_half, s_zero, s_iota = sem("minus_half2_ready"), sem("self_probs_zeroed"), sem("iota_ready")
    s_st, s_rs, s_n2 = sem("norm_stats"), sem("norm_rstd"), sem("self_norm_ready")
    s_t2, s_c2 = sem("self_transposed"), sem("self_t_ready")
    s_ss, s_mx, s_ex, s_pn = sem("self_scores"), sem("self_max_ready"), sem("self_exp"), sem("self_probs_ready")
    s_so, s_acc, s_n3 = sem("self_out"), sem("x_after_self_ready"), sem("ffn_norm_ready")
    s_t3, s_h3, s_l3 = sem("ffn_transposed"), sem("ffn_t_hi"), sem("ffn_t_lo")
    s_lg, s_gt, s_ge = sem("gate_logits_product"), sem("gate_step_done"), sem("gate_exp")
    s_gates = sem("gates_ready")
    s_wl = [[sem(f"w{k + 1}_loaded{i}") for i in range(2)] for k in range(2)]
    s_wh = [sem(f"w{k + 1}_hi_ready") for k in range(2)]
    s_wlo = [sem(f"w{k + 1}_lo_ready") for k in range(2)]
    s_h, s_hf, s_hh, s_hl = sem("hidden_product"), sem("hidden_ready"), sem("hidden_hi"), sem("hidden_lo")
    s_ye, s_yp = sem("ffn_added"), sem("ffn_product")
    s_out = sem("stored")
    s_rc = sem("self_reciprocal")
    s_g1, s_g2, s_g3, s_g4, s_g5 = (sem(f"gate_{n}") for n in ("logits", "top", "index", "weights", "onehot"))

    block = es.enter_context(nc.Block())

    @block.sync
    def _(sp):
        sp.dma_start(wo_f[:], wout.rearrange("(t p) n -> p t n", p=P)).then_inc(s_wo, 16)
        sp.dma_start(gw_f[:], gate_w_t).then_inc(s_gw, 16)

        def load(s, j, first):
            sets = slice(s, s + 1) if isinstance(s, int) else bass.ds(s, 1)
            for k, w in enumerate((w1, w2)):
                if not first:
                    sp.wait_ge(s_wh[k], NJ * s + j - 1)
                    sp.wait_ge(s_wlo[k], NJ * s + j - 1)
                sp.dma_start(wst[k][j % 2][:], w[sets, j].rearrange("o p t h -> p (o t) h")).then_inc(s_wl[k][j % 2], 16)

        for j in range(NJ):
            load(0, j, j < 2)
        with sp.Fori(1, NSETS) as s:
            for j in range(NJ):
                load(s, j, False)
        for i in range(TT):
            sp.wait_ge(s_ye, TT * (NSETS - 1) + i + 1)
            sp.dma_start(out.rearrange("b n d -> (b n) d")[i * P:(i + 1) * P, :], acc[:, i, :]).then_inc(s_out, 16)
        sp.wait_ge(s_out, 16 * TT)

    @block.gpsimd
    def _(pool):
        pool.memset(half[:], -0.5).then_inc(s_half, 1)
        pool.iota(iota8[:], [[1, E]], base=0, channel_multiplier=0, allow_small_or_imprecise_dtypes=True).then_inc(s_iota, 1)
        pool.wait_ge(s_half, 1)
        for n in range(2):
            pool.wait_ge(s_st, 3 * (n + 1))
            pool.tensor_tensor(rstd[:], mv[:, :, 1], half[:], ALU.pow).then_inc(s_rs, 1)

    @block.scalar
    def _(act):
        act.wait_ge(s_wo, 16)
        act.activation(wo[0][:], wo_f[:], ACT.Copy, scale=WEIGHT_SCALE).then_inc(s_woh, 1)
        act.wait_ge(s_gw, 16)
        act.activation(gw[0][:], gw_f[:], ACT.Copy, scale=WEIGHT_SCALE).then_inc(s_woh, 1)
        for i in range(TT):
            act.wait_ge(s_t2, i + 1)
            act.activation(x2T[:, i, :, :], pb[4 + i][:].rearrange("p (t q) -> p t q", q=P), ACT.Copy).then_inc(s_c2, 1)
        act.wait_ge(s_zero, 1)
        for i in range(TT):
            act.wait_ge(s_mx, i + 1)
            for b in range(2):
                r = slice(NQ * b, NQ * b + NQ)
                last = act.activation(pbd[r, i, r], pb[i][r, r], ACT.Exp, bias=smax[r, i:i + 1], accum_out=ssum[r, i:i + 1])
            last.then_inc(s_ex, 1)
        for i in range(TT):
            act.wait_ge(s_t3, i + 1)
            act.activation(x3T[0][:, :, i * P:(i + 1) * P], pb[i][:].rearrange("p (t q) -> p t q", q=P), ACT.Copy).then_inc(s_h3, 1)
        act.wait_ge(s_gt, TT)
        act.activation(gate[:, :, 1], gate[:, :, 0], ACT.Exp).then_inc(s_ge, 1)

        def high(k, s, j):
            act.wait_ge(s_wl[k][j % 2], 16 * (NJ // 2 * s + j // 2 + 1))
            if not (isinstance(s, int) and s == 0 and j < 2):
                act.wait_ge(s_h if k == 0 else s_yp, 4 * (NJ * s + j - 1))
            act.activation(wsp[k][j % 2][0][:], wst[k][j % 2][:], ACT.Copy, scale=WEIGHT_SCALE).then_inc(s_wh[k], 1)

        def hidden(s, j):
            for ht in range(HT):
                n = HT * (NJ * s + j) + ht
                act.wait_ge(s_h, n + 1)
                if not (isinstance(s, int) and s == 0 and j == 0 and ht < 2):
                    act.wait_ge(s_hl, n - 1)
                act.activation(hf[:, ht % 2, :], pb[4 + ht % 2][:], ACT.Silu, scale=UNSCALE).then_inc(s_hf, 1)

        def one_set(s):
            for j in range(NJ):
                high(0, s, j)
                high(1, s, j)
                hidden(s, j)

        one_set(0)
        with act.Fori(1, NSETS) as s:
            one_set(s)

    @block.vector
    def _(dve):
        dve.memset(pbd[:], 0.0).then_inc(s_zero, 1)
        dve.memset(gates[:, :, 0], UNSCALE)
        dve.wait_ge(s_woh, 1)
        for t in range(DT):
            last = dve.scalar_tensor_tensor(wo[1][:, t, :], wo_f[:, t, :], WEIGHT_SCALE, wo[0][:, t, :], ALU.mult, ALU.subtract)
        last.then_inc(s_wol, 1)
        dve.wait_ge(s_woh, 2)
        dve.scalar_tensor_tensor(gw[1][:], gw_f[:], WEIGHT_SCALE, gw[0][:], ALU.mult, ALU.subtract).then_inc(s_wol, 1)
        for i in range(TT):
            dve.wait_ge(s_y, i + 1)
            dve.scalar_tensor_tensor(x1[:, i, :], pb[i][:], UNSCALE, xres[:, i, :], ALU.mult, ALU.add).then_inc(s_x1, 1)

        def layernorm(src, dst, ready, n, done):
            for i in range(TT):
                dve.wait_ge(ready, i + 1)
                last = dve.bn_stats(stats[:, i, :], src[:, i, :])
            last.then_inc(s_st, 1)
            dve.wait_ge(s_st, 3 * n + 1)
            for i in range(TT):
                last = dve.bn_aggr(mv[:, i, :], stats[:, i, :])
            last.then_inc(s_st, 1)
            dve.wait_ge(s_st, 3 * n + 2)
            dve.tensor_scalar(mv[:, :, 1], mv[:, :, 1], EPS, None, ALU.add).then_inc(s_st, 1)
            dve.wait_ge(s_rs, n + 1)
            for i in range(TT):
                dve.tensor_scalar(dst[:, i, :], src[:, i, :], mv[:, i, 0:1], rstd[:, i:i + 1],
                                  ALU.subtract, ALU.mult).then_inc(done, 1)

        layernorm(x1, x2n, s_x1, 0, s_n2)
        for i in range(TT):
            dve.wait_ge(s_ss, i + 1)
            for b in range(2):
                r = slice(NQ * b, NQ * b + NQ)
                last = dve.tensor_reduce(smax[r, i:i + 1], pb[i][r, r], AX.X, ALU.max, negate=True)
            last.then_inc(s_mx, 1)
        for i in range(TT):
            dve.wait_ge(s_ex, i + 1)
            dve.reciprocal(srec[:, i:i + 1], ssum[:, i:i + 1]).then_inc(s_rc, 1)
        for i in range(TT):
            dve.wait_ge(s_rc, i + 1)
            dve.tensor_scalar(pbd[:, i, :], pbd[:, i, :], srec[:, i:i + 1], None, ALU.mult).then_inc(s_pn, 1)
        for i in range(TT):
            dve.wait_ge(s_so, i + 1)
            dve.tensor_tensor(acc[:, i, :], pb[4 + i][:], x1[:, i, :], ALU.add).then_inc(s_acc, 1)
        layernorm(acc, x3n, s_acc, 1, s_n3)
        for i in range(TT):
            c = slice(i * P, (i + 1) * P)
            dve.wait_ge(s_h3, i + 1)
            dve.tensor_tensor(x3T[1][:, :, c], pb[i][:].rearrange("p (t q) -> p t q", q=P), x3T[0][:, :, c], ALU.subtract).then_inc(s_l3, 1)
        for i in range(TT):
            dve.wait_ge(s_lg, i + 1)
            dve.tensor_scalar(logits[:, i, :], pb[4 + i][:, 0:E], UNSCALE, None, ALU.mult).then_inc(s_g1, 1)
        for i in range(TT):
            dve.wait_ge(s_g1, i + 1)
            dve.max(top[:, i, :], logits[:, i, :]).then_inc(s_g2, 1)
        for i in range(TT):
            dve.wait_ge(s_g2, i + 1)
            dve.max_index(topi[:, i, :], top[:, i, :], logits[:, i, :]).then_inc(s_g3, 1)
            dve.tensor_tensor(gate[:, i, 0:1], top[:, i, 1:2], top[:, i, 0:1], ALU.subtract).then_inc(s_gt, 1)
        dve.wait_ge(s_g3, TT)
        dve.tensor_copy(topf[:], topi[:, :, 0:2]).then_inc(s_g4, 1)
        dve.wait_ge(s_ge, 1)
        dve.tensor_scalar(gate[:, :, 2], gate[:, :, 1], 1.0, None, ALU.add).then_inc(s_g4, 1)
        dve.wait_ge(s_g4, 2)
        dve.reciprocal(gate[:, :, 3], gate[:, :, 2]).then_inc(s_g4, 1)
        dve.wait_ge(s_g4, 3)
        dve.tensor_scalar(gate[:, :, 2], gate[:, :, 3], UNSCALE, None, ALU.mult).then_inc(s_g4, 1)
        dve.wait_ge(s_g4, 4)
        dve.tensor_tensor(gate[:, :, 3], gate[:, :, 2], gate[:, :, 1], ALU.mult).then_inc(s_g4, 1)
        dve.wait_ge(s_g4, 5)
        dve.wait_ge(s_iota, 1)
        for i in range(TT):
            dve.tensor_scalar(g1hot[:, i, :], iota8[:], topf[:, i, 1:2], gate[:, i, 3:4], ALU.is_equal, ALU.mult)
            dve.tensor_scalar(gates[:, i, 1:1 + E], iota8[:], topf[:, i, 0:1], gate[:, i, 2:3], ALU.is_equal, ALU.mult).then_inc(s_g5, 1)
        dve.wait_ge(s_g5, TT)
        dve.tensor_tensor(gates[:, :, 1:1 + E], gates[:, :, 1:1 + E], g1hot[:], ALU.add).then_inc(s_gates, 1)
        dve.wait_ge(s_gates, 1)

        def low(k, s, j):
            dve.wait_ge(s_wh[k], NJ * s + j + 1)
            for t in range(4):
                last = dve.scalar_tensor_tensor(wsp[k][j % 2][1][:, t, :], wst[k][j % 2][:, t, :], WEIGHT_SCALE,
                                                wsp[k][j % 2][0][:, t, :], ALU.mult, ALU.subtract)
            last.then_inc(s_wlo[k], 1)

        def hidden(s, j):
            for ht in range(HT):
                n = HT * (NJ * s + j) + ht
                dve.wait_ge(s_hf, n + 1)
                if not (isinstance(s, int) and s == 0 and j < 2):
                    dve.wait_ge(s_yp, TT * (NJ * s + j - 1))
                dve.tensor_copy(hT[j % 2][0][:, ht, :], hf[:, ht % 2, :]).then_inc(s_hh, 1)
                dve.wait_ge(s_hh, n + 1)
                dve.tensor_tensor(hT[j % 2][1][:, ht, :], hf[:, ht % 2, :], hT[j % 2][0][:, ht, :], ALU.subtract).then_inc(s_hl, 1)

        def one_set(s):
            for j in range(NJ):
                low(0, s, j)
                low(1, s, j)
                hidden(s, j)
            sets = slice(s, s + 1) if isinstance(s, int) else bass.ds(s, 1)
            for i in range(TT):
                dve.wait_ge(s_yp, TT * (NJ * s + NJ - 1) + i + 1)
                if not (isinstance(s, int) and s == 0):
                    dve.wait_ge(s_ye, TT * (s - 1) + i + 1)
                dve.scalar_tensor_tensor(acc[:, i, :], pb[i][:], gates[:, i, sets], acc[:, i, :], ALU.mult, ALU.add).then_inc(s_ye, 1)

        one_set(0)
        with dve.Fori(1, NSETS) as s:
            one_set(s)

    @block.tensor
    def _(pe):
        def product(out_, lhs, rhs, first, last):
            pe.matmul(out_, lhs[0], rhs[0], start=first, stop=False)
            pe.matmul(out_, lhs[0], rhs[1], start=False, stop=False)
            return pe.matmul(out_, lhs[1], rhs[0], start=False, stop=last)

        pe.wait_ge(s_wol, 1)
        for i in range(TT):
            for t in range(DT):
                last = product(pb[i][:], [o[:, t, i * P:(i + 1) * P] for o in oT], [w[:, t, :] for w in wo], t == 0, t == DT - 1)
            last.then_inc(s_y, 1)
        for i in range(TT):
            pe.wait_ge(s_n2, i + 1)
            for dt in range(DT):
                last = pe.transpose(pb[4 + i][:, dt * P:(dt + 1) * P], x2n[:, i, dt * P:(dt + 1) * P], ident[:])
            last.then_inc(s_t2, 1)
        for i in range(TT):
            pe.wait_ge(s_c2, i + 1)
            pe.wait_ge(s_x1, i + 1)
            for dt in range(DT):
                last = pe.matmul(pb[i][:, 0:P], x2T[:, i, dt, :], x2T[:, i, dt, :], start=dt == 0, stop=dt == DT - 1)
            last.then_inc(s_ss, 1)
        for i in range(TT):
            pe.wait_ge(s_pn, i + 1)
            pe.matmul(pb[4 + i][:], pbd[:, i, :], x2n[:, i, :], start=True, stop=True).then_inc(s_so, 1)
        for i in range(TT):
            pe.wait_ge(s_n3, i + 1)
            for dt in range(DT):
                last = pe.transpose(pb[i][:, dt * P:(dt + 1) * P], x3n[:, i, dt * P:(dt + 1) * P], ident[:])
            last.then_inc(s_t3, 1)
        pe.wait_ge(s_wol, 2)
        for i in range(TT):
            pe.wait_ge(s_l3, i + 1)
            for dt in range(DT):
                last = product(pb[4 + i][:, 0:E], [v[:, dt, i * P:(i + 1) * P] for v in x3T], [g[:, dt, :] for g in gw], dt == 0, dt == DT - 1)
            last.then_inc(s_lg, 1)
        pe.wait_ge(s_g1, TT)

        def hidden(s, j):
            pe.wait_ge(s_wlo[0], NJ * s + j + 1)
            for ht in range(HT):
                if not (isinstance(s, int) and s == 0 and j == 0 and ht < 2):
                    pe.wait_ge(s_hf, HT * (NJ * s + j) + ht - 1)
                for dt in range(DT):
                    last = product(pb[4 + ht % 2][:], [w[:, dt, ht * P:(ht + 1) * P] for w in wsp[0][j % 2]], [v[:, dt, :] for v in x3T], dt == 0, dt == DT - 1)
                last.then_inc(s_h, 1)

        def output(s, j):
            pe.wait_ge(s_wlo[1], NJ * s + j + 1)
            pe.wait_ge(s_hl, HT * (NJ * s + j) + HT)
            for i in range(TT):
                if j == 0 and not (isinstance(s, int) and s == 0):
                    pe.wait_ge(s_ye, TT * (s - 1) + i + 1)
                for ht in range(HT):
                    last = product(pb[i][:], [h[:, ht, i * P:(i + 1) * P] for h in hT[j % 2]], [w[:, ht, :] for w in wsp[1][j % 2]],
                                   j == 0 and ht == 0, j == NJ - 1 and ht == HT - 1)
                last.then_inc(s_yp, 1)

        def one_set(s):
            hidden(s, 0)
            for j in range(1, NJ):
                hidden(s, j)
                output(s, j - 1)
            output(s, NJ - 1)

        one_set(0)
        with pe.Fori(1, NSETS) as s:
            one_set(s)


def kernel(x, ctx_1024, mask_BxS2_bk0, L0_xattn_kv_gate, L0_xattn_gamma_media, L0_xattn_beta_media, L0_xattn_gamma_lat,
           L0_xattn_beta_lat, L0_xattn_Wq, L0_xattn_Wk, L0_xattn_Wv, L0_xattn_Wout, L0_ffn_shared_w1, L0_ffn_shared_w2,
           L0_ffn_experts_w1, L0_ffn_experts_w2, L0_ffn_gate_w):
    import numpy as np
    import concourse.bacc as bacc
    from concourse.bass_utils import run_bass_kernel_spmd

    nc = bacc.Bacc("TRN2", target_bir_lowering=False, num_devices=1)
    arrays = {}

    def given(name, a):
        arrays[name] = np.ascontiguousarray(a)
        return nc.dram_tensor(name, arrays[name].shape, mybir.dt.from_np(arrays[name].dtype), kind="ExternalInput").ap()

    D = x.shape[2]
    DT = D // P
    HC = 512
    w1 = np.concatenate([np.asarray(L0_ffn_shared_w1)[None], np.asarray(L0_ffn_experts_w1)])
    w2 = np.concatenate([np.asarray(L0_ffn_shared_w2)[None], np.asarray(L0_ffn_experts_w2)])
    sets, hidden, _ = w1.shape
    w1 = w1.reshape(sets, hidden // HC, HC, DT, P).transpose(0, 1, 4, 3, 2)
    w2 = w2.reshape(sets, D, hidden // HC, HC // P, P).transpose(0, 2, 4, 3, 1)
    gate_w = np.asarray(L0_ffn_gate_w)
    gamma_media = np.asarray(L0_xattn_gamma_media)
    out = nc.dram_tensor("out", tuple(x.shape), F32, kind="ExternalOutput").ap()
    perceiver_kernel(
        nc,
        x=given("x", np.asarray(x)),
        ctx_in=given("ctx", np.asarray(ctx_1024)),
        mask=given("mask", np.asarray(mask_BxS2_bk0)),
        kv_gate=given("kv_gate", np.asarray(L0_xattn_kv_gate).reshape(1, 1)),
        gamma_media=given("gamma_media", gamma_media.reshape(1, D)),
        beta_media=given("beta_media", np.asarray(L0_xattn_beta_media).reshape(1, D)),
        gamma_media_cols=given("gamma_media_cols", gamma_media.reshape(DT, P).T),
        gamma_lat=given("gamma_lat", np.asarray(L0_xattn_gamma_lat).reshape(1, D)),
        beta_lat=given("beta_lat", np.asarray(L0_xattn_beta_lat).reshape(1, D)),
        wq=given("wq", np.asarray(L0_xattn_Wq)),
        wk_t=given("wk_t", np.asarray(L0_xattn_Wk).T),
        wv=given("wv", np.asarray(L0_xattn_Wv)),
        wout=given("wout", np.asarray(L0_xattn_Wout)),
        w1=given("w1", w1),
        w2=given("w2", w2),
        gate_w_t=given("gate_w_t", gate_w.reshape(gate_w.shape[0], DT, P).transpose(2, 1, 0)),
        kv_latents=nc.dram_tensor("kv_latents", (x.shape[0] * x.shape[1], D), F32, kind="Internal").ap(),
        out=out,
    )
    r = run_bass_kernel_spmd(nc, [arrays], core_ids=[0])
    return r.results[0]["out"]
```

```python
from contextlib import ExitStack

import concourse.bass as bass
from concourse import mybir

F32 = mybir.dt.float32
F16 = mybir.dt.float16
U8 = mybir.dt.uint8
U32 = mybir.dt.uint32
I32 = mybir.dt.int32
ALU = mybir.AluOpType
ACT = mybir.ActivationFunctionType
AX = mybir.AxisListType

P = 128
EPS = 1e-5
WEIGHT_SCALE = 256.0
UNSCALE = 1.0 / WEIGHT_SCALE
MASKED = -1e30
LOWEST = -3.0e38


def perceiver_kernel(nc, x, ctx_in, mask, kv_gate, gamma_media, beta_media, gamma_media_cols, gamma_lat, beta_lat,
                     wq, wk_t, wv, wout, w1, w2, gate_w_t, kv_latents, out):
    B, NQ, D = x.shape
    F = ctx_in.shape[1]
    HEADS = 8
    DH = D // HEADS
    DT = D // P
    TOK = B * NQ
    TT = TOK // P
    HQ_TILES = HEADS * NQ // P
    SCALE = float(DH) ** -0.5
    FULL = F // P
    REM = F - FULL * P
    MT = FULL + 1
    KT = MT + 1
    LAT = MT
    KEYS = F + NQ
    CHUNKS = 4
    CH = KEYS // CHUNKS
    LAST = KEYS - (CHUNKS - 1) * CH
    LAST_MEDIA = LAST - NQ
    assert LAST <= 512 and FULL == 12 and DT == 4 and HQ_TILES == 4 and TT == 4

    es = ExitStack()
    first_half = ExitStack()
    with es:
        def keep(name, shape, dt):
            return es.enter_context(nc.sbuf_tensor(name, shape, dt))

        def sb(name, shape, dt):
            return first_half.enter_context(nc.sbuf_tensor(name, shape, dt))

        def sem(name):
            return es.enter_context(nc.semaphore(name))

        xres = keep("residual", [P, TT, D], F32)
        oT = [keep("heads_t_hi", [P, HQ_TILES, TOK], F16), keep("heads_t_lo", [P, HQ_TILES, TOK], F16)]
        ident = keep("ident", [P, P], F32)
        E = gate_w_t.shape[2]
        wo = [keep("wout_hi", [P, DT, D], F16), keep("wout_lo", [P, DT, D], F16)]
        gw = [keep("gate_w_hi", [P, DT, E], F16), keep("gate_w_lo", [P, DT, E], F16)]
        wo_f = sb("wout_f32", [P, DT, D], F32)
        gw_f = sb("gate_w_f32", [P, DT, E], F32)
        xs = sb("media_f32", [P, KT, D], F32)
        xn = [sb("media_rows_hi", [P, KT, D], F16), sb("media_rows_lo", [P, KT, D], F16)]
        xT = [sb("media_cols_hi", [P, DT, KEYS + 1], F16), sb("media_cols_lo", [P, DT, KEYS + 1], F16)]
        TWICE = KEYS + NQ
        probs_all = sb("probs", [P, 2 * TWICE], F32)
        probs = [probs_all[:, i * TWICE:(i + 1) * TWICE] for i in range(2)]
        pT_all = sb("probs_t", [P, 4 * KT * P], F16)
        pT = [[pT_all[:, (2 * i + h) * KT * P:(2 * i + h + 1) * KT * P].rearrange("p (k q) -> p k q", q=P) for h in range(2)]
              for i in range(2)]
        qp_all = sb("q_keyspace", [P, 2 * DT * 512], F16)
        qp = [qp_all[:, h * DT * 512:(h + 1) * DT * 512].rearrange("p (t q) -> p t q", q=512) for h in range(2)]
        wk = [sb("wk_t_hi", [P, DT, D], F16), sb("wk_t_lo", [P, DT, D], F16)]
        wvs = [sb("wv_hi", [P, DT, D], F16), sb("wv_lo", [P, DT, D], F16)]
        qbd = [sb("q_blockdiag_hi", [P, B, HQ_TILES, P], F16), sb("q_blockdiag_lo", [P, B, HQ_TILES, P], F16)]
        qnow = [sb("q_now_hi", [P, HQ_TILES, P], F16), sb("q_now_lo", [P, HQ_TILES, P], F16)]
        mask_u8 = sb("mask_u8", [P, F], U8)
        mask_f = sb("mask_bias", [P, F], F32)
        gm_bc = sb("gamma_media_bc", [P, D], F32)
        bm_bc = sb("beta_media_bc", [P, D], F32)
        gm_col = sb("gamma_media_col", [P, DT], F32)
        gate_c = sb("kv_gate_col", [P, 1], F32)
        usb = sb("u_rows", [P, 2, D], F32)
        uT = [sb("u_cols_hi", [P, DT, P], F16), sb("u_cols_lo", [P, DT, P], F16)]
        stats = sb("stats", [P, MT, 6], F32)
        mv = sb("mean_var", [P, MT, 2], F32)
        rstd = sb("rstd", [P, MT], F32)
        half = sb("minus_half", [P, MT], F32)
        shift = sb("minus_mean_rstd", [P, MT], F32)
        masked = sb("masked_bias", [P, 1], F32)
        bk = sb("beta_wk", [P, DT], F32)
        bkh = [sb("beta_wk_hi", [P, DT], F16), sb("beta_wk_lo", [P, DT], F16)]
        qb_all = sb("q_beta_all", [P, B * HQ_TILES], F32)
        qb_now = sb("q_beta_now", [P, HQ_TILES], F32)
        cmax = sb("chunk_max", [P, 2, 8], F32)
        rmax = sb("row_max", [P, 2, 4], F32)
        rsum = sb("row_sum", [P, 2, 4], F32)
        unorm = sb("u_norm", [P, 4], F32)
        spare = sb("spare", [P, 1 + HQ_TILES * CHUNKS], F32)
        pool_spare = sb("pool_spare", [P, 1], F32)
        psim = [first_half.enter_context(nc.psum_tensor(f"p_sim{i}", [P, 512], F32)) for i in range(CHUNKS)]
        ptp = [first_half.enter_context(nc.psum_tensor(f"p_tp{i}", [P, 512], F32)) for i in range(2)]
        pum = first_half.enter_context(nc.psum_tensor("p_u_media", [P, 512], F32))
        pul = first_half.enter_context(nc.psum_tensor("p_u_latent", [P, 512], F32))

        lat = xT[0][:, :, :].rearrange("p a b -> p (a b)").bitcast(F32)[:, 0:TT * D].rearrange("p (t d) -> p t d", t=TT)
        kvl = xT[1][:, :, :].rearrange("p a b -> p (a b)").bitcast(F32)[:, 0:TT * D].rearrange("p (t d) -> p t d", t=TT)
        wq_f = pT_all[:].bitcast(F32)[:, 0:DT * D].rearrange("p (t d) -> p t d", t=DT)
        wk_f = probs_all[:, 0:DT * D].rearrange("p (t d) -> p t d", t=DT)
        wv_f = wo_f[:]
        gl_bc = pT_all[:].bitcast(F32)[:, DT * D:(DT + 1) * D]
        bl_bc = probs_all[:, DT * D:(DT + 1) * D]
        latT = [xn[h][:, 0:4, :] for h in range(2)]
        wqs = [xn[h][:, 4:8, :] for h in range(2)]

        s_xin, s_aff, s_wq, s_wk, s_wv = sem("x_loaded"), sem("affine_loaded"), sem("wq_loaded"), sem("wk_loaded"), sem("wv_loaded")
        s_id, s_half, s_zero = sem("ident_ready"), sem("minus_half_ready"), sem("q_blockdiag_zeroed")
        s_st = sem("setup_stats")
        s_rs, s_lr, s_bt, s_qbn = sem("setup_rstd"), sem("latents_step"), sem("beta_step"), sem("q_beta_now_ready")
        s_lat = sem("latents_ready")
        s_kvl, s_kvst = sem("kv_latents_ready"), sem("kv_latents_stored")
        s_xz = sem("media_padding_zeroed")
        s_whi, s_wlo = sem("weights_hi"), sem("weights_lo")
        s_ltp, s_lhi, s_llo = sem("latents_transposed"), sem("latents_t_hi"), sem("latents_t_lo")
        s_qp, s_qhi, s_qlo = sem("q_product"), sem("q_hi"), sem("q_lo")
        s_bk, s_qb, s_qbs = sem("beta_wk_ready"), sem("q_beta_product"), sem("q_beta_ready")
        s_wo, s_woh, s_wol = sem("wout_gate_w_loaded"), sem("wout_hi_ready"), sem("wout_lo_ready")
        s_ctx, s_mk = sem("ctx_loaded"), sem("mask_loaded")
        s_mc, s_mf = sem("mask_as_float"), sem("mask_ready")
        s_bs, s_ve, s_rd = sem("media_stats"), sem("media_var"), sem("media_rstd")
        s_shift, s_norm0, s_norm = sem("first_shift_ready"), sem("first_media_normalised"), sem("media_normalised")
        s_nh, s_nl = sem("media_rows_hi_ready"), sem("media_rows_lo_ready")
        s_qn = sem("q_now_ready")
        s_sim, s_sfree = sem("sim_ready"), sem("sim_free")
        s_rm, s_exp = sem("row_max_step"), sem("probs_ready")
        s_tp, s_thi, s_tfree = sem("tp_ready"), sem("tp_hi"), sem("tp_free")
        s_xp, s_xhi, s_xfree = sem("prep_ready"), sem("prep_hi"), sem("prep_free")
        s_pv, s_u = sem("pv_ready"), sem("u_step")

        AFTER = [{3: [("P", 0, 2)], 7: [("P", 0, 3)]},
                 {1: [("U", 0)], 3: [("P", 1, 2)], 7: [("P", 1, 3)], 10: [("V", 0)]},
                 {1: [("U", 1)], 3: [("P", 2, 2)], 5: [("x", 0)], 6: [("x", 1)], 7: [("P", 2, 3)], 8: [("x", 2)],
                  9: [("x", 3)], 10: [("V", 1), ("x", 4)], 11: [("x", 5)], 12: [("P", 3, 0), ("x", 6)],
                  13: [("P", 3, 1), ("x", 7)]},
                 {0: [("x", 8)], 1: [("x", 9)], 2: [("x", 10)], 3: [("P", 3, 2)], 4: [("U", 2)], 5: [("x", 11)],
                  6: [("x", 12), ("x", 13)], 7: [("P", 3, 3)], 8: [("q", 0)], 9: [("q", 1)], 10: [("V", 2), ("q", 2)],
                  11: [("q", 3)]}]
        ROUNDS = 24
        XROUNDS = FULL + 2
        PREP = [("x", i) for i in range(XROUNDS)] + [("q", i) for i in range(DT)]
        NPREP = len(PREP)
        ACT_TILES = 8
        GROUPS = [(range(0, 4), PREP[0:4]), (range(4, 8), PREP[4:8]), (range(8, MT), PREP[8:XROUNDS])]

        def kept(rounds, last):
            return [r for r in rounds if not (last and r[0] in "xq")]

        def cells(t, last, tiles=range(KT)):
            return kept([r for k in tiles for r in AFTER[t].get(k, [])], last)

        def media_bank(t):
            return psim[3] if t == HQ_TILES - 1 else pum

        def rows(k):
            return P if k < FULL else REM

        block = first_half.enter_context(nc.Block())

        @block.sync
        def _(sp):
            def one(b):
                return bass.ds(b, 1) if not isinstance(b, int) else slice(b, b + 1)

            def load_media(b):
                sp.dma_start(xs[:, 0:FULL, :], ctx_in[one(b), 0:FULL * P, :].rearrange("o (t p) d -> p (o t) d", p=P)).then_inc(s_ctx, 16)
                sp.dma_start(xs[0:REM, FULL, :], ctx_in[one(b), FULL * P:F, :].rearrange("o p d -> (o p) d")).then_inc(s_ctx, 16)

            def load_latents(b):
                rows_of_b = kv_latents.rearrange("(b n) d -> b n d", n=NQ)[one(b), :, :]
                for r in range(0, P, NQ):
                    sp.dma_start(xs[r:r + NQ, LAT, :], rows_of_b.rearrange("o p d -> (o p) d")).then_inc(s_ctx, 16)

            def load_mask(b):
                sp.dma_start(mask_u8[:, :], mask[one(b), :].broadcast_to((P, F))).then_inc(s_mk, 16)

            sp.dma_start(xres[:], x.rearrange("b n d -> (b n) d").rearrange("(t p) d -> p t d", p=P)).then_inc(s_xin, 16)
            sp.dma_start(wq_f, wq.rearrange("(t p) n -> p t n", p=P)).then_inc(s_wq, 16)
            sp.dma_start(wk_f, wk_t.rearrange("(t p) n -> p t n", p=P)).then_inc(s_wk, 16)
            sp.wait_ge(s_xz, 1)
            load_media(0)
            sp.dma_start(wv_f, wv.rearrange("(t p) n -> p t n", p=P)).then_inc(s_wv, 16)
            load_mask(0)
            sp.wait_ge(s_kvl, TT)
            sp.dma_start(kv_latents.rearrange("(t p) d -> p t d", p=P), kvl).then_inc(s_kvst, 16)
            sp.wait_ge(s_kvst, 16)
            sp.wait_ge(s_ctx, 32)
            load_latents(0)
            sp.wait_ge(s_wlo, 3)
            sp.dma_start(wo_f[:], wout.rearrange("(t p) n -> p t n", p=P)).then_inc(s_wo, 16)
            sp.dma_start(gw_f[:], gate_w_t).then_inc(s_wo, 16)
            with sp.Fori(1, B) as b:
                sp.wait_ge(s_nh, KT * b)
                sp.wait_ge(s_nl, KT * b)
                sp.wait_ge(s_mf, b)
                load_media(b)
                load_latents(b)
                load_mask(b)

        @block.gpsimd
        def _(pool):
            pool.dma_start(gl_bc, gamma_lat.broadcast_to((P, D))).then_inc(s_aff, 16)
            pool.dma_start(bl_bc, beta_lat.broadcast_to((P, D))).then_inc(s_aff, 16)
            pool.dma_start(gm_bc[:], gamma_media.broadcast_to((P, D))).then_inc(s_aff, 16)
            pool.dma_start(bm_bc[:], beta_media.broadcast_to((P, D))).then_inc(s_aff, 16)
            pool.dma_start(gm_col[:], gamma_media_cols).then_inc(s_aff, 16)
            pool.dma_start(gate_c[:], kv_gate.broadcast_to((P, 1))).then_inc(s_aff, 16)
            pool.memset(xs[:, FULL:KT, :], 0.0).then_inc(s_xz, 1)
            pool.memset(ident[:], 0.0).then_inc(s_id, 1)
            pool.memset(masked[:], MASKED).then_inc(s_half, 1)
            pool.memset(half[:], -0.5).then_inc(s_half, 1)
            pool.wait_ge(s_id, 1)
            pool.affine_select(out=ident[:], in_=ident[:], compare_op=ALU.not_equal, fill=1.0, base=0,
                               pattern=[[-1, P]], channel_multiplier=1).then_inc(s_id, 1)
            pool.wait_ge(s_half, 2)
            for n in range(2):
                pool.wait_ge(s_st, 3 * (n + 1))
                pool.tensor_tensor(rstd[:, 0:TT], mv[:, 0:TT, 1], half[:, 0:TT], ALU.pow).then_inc(s_rs, 1)
                if n == 1:
                    pool.memset(qbd[0][:], 0.0)
                    pool.memset(qbd[1][:], 0.0).then_inc(s_zero, 1)

            def media_rstd(n):
                pool.wait_ge(s_ve, n)
                pool.tensor_tensor(rstd[:], mv[:, :, 1], half[:], ALU.pow).then_inc(s_rd, 1)

            def mask_bias(b1):
                pool.wait_ge(s_mk, b1 * 16)
                pool.tensor_tensor(pool_spare[:], masked[:], masked[:], ALU.add)
                pool.tensor_copy(mask_f[:], mask_u8[:]).then_inc(s_mc, 1)
                pool.wait_ge(s_mc, b1)
                pool.tensor_tensor(mask_f[:], mask_f[:], masked[:, 0:1].broadcast_to((P, F)), ALU.mult).then_inc(s_mf, 1)

            media_rstd(1)
            mask_bias(1)
            with pool.Fori(1, B) as b:
                media_rstd(b + 1)
                pool.wait_ge(s_sfree, CHUNKS * HQ_TILES * b)
                mask_bias(b + 1)

        @block.scalar
        def _(act):
            def split_hi(out_, in_, scale=1.0):
                return act.activation(out_, in_, ACT.Copy, scale=scale)

            act.wait_ge(s_wq, 16)
            split_hi(wqs[0], wq_f, WEIGHT_SCALE).then_inc(s_whi, 1)
            act.wait_ge(s_wk, 16)
            split_hi(wk[0][:], wk_f, WEIGHT_SCALE).then_inc(s_whi, 1)
            act.wait_ge(s_aff, 96)
            for t in range(TT):
                act.wait_ge(s_lat, t + 1)
                split_hi(kvl[:, t, :], lat[:, t, :], gate_c[:, 0:1]).then_inc(s_kvl, 1)
            for dt in range(DT):
                act.wait_ge(s_ltp, dt + 1)
                split_hi(latT[0][:, dt, :], psim[dt][:]).then_inc(s_lhi, 1)
            rnd = [0]

            def take(kind, b):
                if kind[0] in "xq":
                    r = PREP.index(kind)
                    p, done = psim[r % 3], s_xhi
                    act.wait_ge(s_xp, NPREP * b + r + 1)
                else:
                    r = rnd[0]
                    rnd[0] += 1
                    p, done = ptp[r % 2], s_thi
                    act.wait_ge(s_tp, ROUNDS * b + r + 1)
                if kind[0] == "P":
                    dst = pT[kind[1] % 2][0]
                    if kind[2] < 3:
                        split_hi(dst[:, 4 * kind[2]:4 * kind[2] + 4, :], p[:].rearrange("p (k q) -> p k q", q=P)).then_inc(done, 1)
                    else:
                        split_hi(dst[0:REM, FULL, :], p[0:REM, 0:P])
                        split_hi(dst[:, LAT, :], p[:, P:2 * P]).then_inc(done, 1)
                elif kind[0] == "x":
                    i = kind[1]
                    if i < 12:
                        act.activation(xT[0][:, i % 4, (i // 4) * 512:(i // 4) * 512 + 512], p[:], ACT.Copy,
                                       scale=gm_col[:, i % 4:i % 4 + 1]).then_inc(done, 1)
                    elif i == 12:
                        for dt in range(DT):
                            last = act.activation(xT[0][:, dt, FULL * P:F], p[:, dt * REM:(dt + 1) * REM], ACT.Copy,
                                                  scale=gm_col[:, dt:dt + 1])
                        last.then_inc(done, 1)
                    else:
                        split_hi(xT[0][:, :, F:KEYS], p[:].rearrange("p (t q) -> p t q", t=DT)[:, :, 0:NQ]).then_inc(done, 1)
                elif kind[0] == "q":
                    split_hi(qp[0][:, kind[1], :], p[:], UNSCALE).then_inc(done, 1)
                elif kind[0] == "U":
                    split_hi(uT[0][:], p[:].rearrange("p (t q) -> p t q", t=DT)).then_inc(done, 1)
                else:
                    for i in range(2):
                        s = slice(64 * i, 64 * i + 64)
                        last = split_hi(oT[0][s, kind[1], bass.ds(b * NQ, NQ)], p[s, 64 * i:64 * i + 64], UNSCALE)
                    last.then_inc(done, 1)

            def exponentials(t, b):
                act.wait_ge(s_rm, 4 * (HQ_TILES * b + t) + 4)
                pr = probs[t % 2]
                act.activation(pr[:, 0:F], pr[:, 0:F], ACT.Exp, bias=rmax[:, t % 2, 3:4],
                               accum_out=rsum[:, t % 2, 0:1])
                act.activation(pr[:, KEYS:TWICE], pr[:, F:KEYS], ACT.Exp, bias=rmax[:, t % 2, 2:3])
                act.activation(pr[:, F:KEYS], pr[:, F:KEYS], ACT.Exp, bias=rmax[:, t % 2, 2:3],
                               accum_out=rsum[:, t % 2, 1:2]).then_inc(s_exp, 1)

            act.wait_ge(s_zero, 1)
            for t in range(HQ_TILES):
                act.wait_ge(s_qp, t + 1)
                for i in range(2):
                    src = [*ptp, pum, pul][t][64 * i:64 * i + 64, :].rearrange("p (b n) -> p b n", n=NQ)
                    last = split_hi(qbd[0][64 * i:64 * i + 64, :, t, 64 * i:64 * i + 64], src, UNSCALE)
                last.then_inc(s_qhi, 1)

            act.wait_ge(s_shift, 1)
            for tiles, rounds in GROUPS:
                for k in range(tiles.start, min(tiles.stop, ACT_TILES)):
                    act.activation(xs[:, k, :], xs[:, k, :], ACT.Identity, scale=rstd[:, k:k + 1], bias=shift[:, k:k + 1]).then_inc(s_norm0, 1)
                for r in rounds:
                    take(r, 0)
            for r in PREP[XROUNDS:]:
                take(r, 0)
            act.wait_ge(s_wv, 16)
            split_hi(wvs[0][:], wv_f, WEIGHT_SCALE).then_inc(s_whi, 1)

            def row_high(b, first):
                if first:
                    act.wait_ge(s_norm0, ACT_TILES)
                act.wait_ge(s_norm, MT * (b + 1) - ACT_TILES)
                act.wait_ge(s_ctx, 64 * (b + 1))
                if not first:
                    act.wait_ge(s_pv, HQ_TILES * b)
                for k in range(MT):
                    split_hi(xn[0][:, k, :], xs[:, k, :]).then_inc(s_nh, 1)
                split_hi(xn[0][0:NQ, LAT, :], xs[0:NQ, LAT, :])
                split_hi(xn[1][NQ:P, LAT, :], xs[NQ:P, LAT, :]).then_inc(s_nh, 1)

            def batch(b, first, last):
                row_high(b, first)
                if not first:
                    rnd[0] = ROUNDS - 2
                    take(("U", 3), b - 1)
                exponentials(0, b)
                if not first:
                    take(("V", 3), b - 1)
                rnd[0] = 0
                take(("P", 0, 0), b)
                take(("P", 0, 1), b)
                exponentials(1, b)
                if last:
                    act.wait_ge(s_wo, 32)
                    split_hi(wo[0][:], wo_f[:], WEIGHT_SCALE).then_inc(s_woh, 1)
                    split_hi(gw[0][:], gw_f[:], WEIGHT_SCALE).then_inc(s_woh, 1)
                for r in cells(0, last):
                    take(r, b)
                for t in (1, 2):
                    take(("P", t, 0), b)
                    take(("P", t, 1), b)
                    exponentials(t + 1, b)
                    for r in cells(t, last):
                        take(r, b + 1 if r[0] in "xq" else b)
                for r in cells(3, last):
                    take(r, b + 1 if r[0] in "xq" else b)

            batch(0, True, False)
            with act.Fori(1, B - 1) as b:
                batch(b, False, False)
            batch(B - 1, False, True)
            take(("U", 3), B - 1)
            take(("V", 3), B - 1)

        @block.vector
        def _(dve):
            def split_lo(out_, in_, hi, scale=1.0):
                return dve.scalar_tensor_tensor(out_, in_, scale, hi, ALU.mult, ALU.subtract)

            dve.wait_ge(s_xin, 16)
            for rep, src in ((0, xres), (1, lat)):
                for t in range(TT):
                    last = dve.bn_stats(stats[:, t, :], src[:, t, :])
                last.then_inc(s_st, 1)
                dve.wait_ge(s_st, 3 * rep + 1)
                if rep:
                    dve.wait_ge(s_rs, 1)
                for t in range(TT):
                    last = dve.bn_aggr(mv[:, t, :], stats[:, t, :])
                last.then_inc(s_st, 1)
                dve.wait_ge(s_st, 3 * rep + 2)
                dve.tensor_scalar(mv[:, 0:TT, 1], mv[:, 0:TT, 1], EPS, None, ALU.add).then_inc(s_st, 1)
                if rep == 0:
                    dve.wait_ge(s_rs, 1)
                    for t in range(TT):
                        last = dve.tensor_scalar(lat[:, t, :], src[:, t, :], mv[:, t, 0:1], rstd[:, t:t + 1], ALU.subtract, ALU.mult)
                    last.then_inc(s_lr, 1)
                    dve.wait_ge(s_lr, 1)
            dve.wait_ge(s_aff, 96)
            for t in range(TT):
                last = dve.scalar_tensor_tensor(lat[:, t, :], lat[:, t, :], mv[:, t, 0:1], gl_bc, ALU.subtract, ALU.mult)
            last.then_inc(s_lr, 1)
            dve.wait_ge(s_lr, 2)
            dve.wait_ge(s_rs, 2)
            for t in range(TT):
                dve.scalar_tensor_tensor(lat[:, t, :], lat[:, t, :], rstd[:, t:t + 1], bl_bc, ALU.mult, ALU.add).then_inc(s_lat, 1)

            def weight_low(n, w, f):
                dve.wait_ge(s_whi, n)
                for dt in range(DT):
                    last = split_lo(w[1][:, dt, :], f[:, dt, :], w[0][:, dt, :], WEIGHT_SCALE)
                last.then_inc(s_wlo, 1)

            def media_stats(b1, tiles):
                if 0 in tiles:
                    dve.wait_ge(s_ctx, 32 if isinstance(b1, int) and b1 == 1 else 64 * b1)
                for k in tiles:
                    last = dve.bn_stats(stats[:, k, :], xs[:, k, :])
                if MT - 1 not in tiles:
                    return
                last.then_inc(s_bs, 1)
                dve.wait_ge(s_bs, 2 * b1 - 1)
                dve.tensor_copy(spare[:, 0:1], stats[:, MT - 1, 0:1])
                for k in range(MT):
                    last = dve.bn_aggr(mv[:, k, :], stats[:, k, :])
                last.then_inc(s_bs, 1)
                dve.wait_ge(s_bs, 2 * b1)
                dve.tensor_scalar(mv[:, :, 1], mv[:, :, 1], EPS, None, ALU.add).then_inc(s_ve, 1)

            def queries(b):
                for h in range(2):
                    last = dve.tensor_copy(qnow[h][:], qbd[h][:, bass.ds(b, 1), :, :].rearrange("p o t q -> p (o t) q"))
                last.then_inc(s_qn, 1)

            rnd = [0]

            def take(kind, b):
                if kind[0] in "xq":
                    r = PREP.index(kind)
                    p, done = psim[r % 3], s_xfree
                    dve.wait_ge(s_xhi, NPREP * b + r + 1)
                else:
                    r = rnd[0]
                    rnd[0] += 1
                    p, done = ptp[r % 2], s_tfree
                    dve.wait_ge(s_thi, ROUNDS * b + r + 1)
                if kind[0] == "P":
                    hi, lo = pT[kind[1] % 2]
                    if kind[2] < 3:
                        s = slice(4 * kind[2], 4 * kind[2] + 4)
                        split_lo(lo[:, s, :], p[:].rearrange("p (k q) -> p k q", q=P), hi[:, s, :]).then_inc(done, 1)
                    else:
                        split_lo(lo[0:REM, FULL, :], p[0:REM, 0:P], hi[0:REM, FULL, :])
                        split_lo(lo[0:NQ, LAT, :], p[0:NQ, P:2 * P], hi[0:NQ, LAT, :]).then_inc(done, 1)
                elif kind[0] == "x":
                    i = kind[1]
                    if i < 12:
                        s = slice((i // 4) * 512, (i // 4) * 512 + 512)
                        split_lo(xT[1][:, i % 4, s], p[:], xT[0][:, i % 4, s], gm_col[:, i % 4:i % 4 + 1]).then_inc(done, 1)
                    elif i == 12:
                        for dt in range(DT):
                            last = split_lo(xT[1][:, dt, FULL * P:F], p[:, dt * REM:(dt + 1) * REM],
                                            xT[0][:, dt, FULL * P:F], gm_col[:, dt:dt + 1])
                        last.then_inc(done, 1)
                    else:
                        split_lo(xT[1][:, :, F:KEYS], p[:].rearrange("p (t q) -> p t q", t=DT)[:, :, 0:NQ],
                                 xT[0][:, :, F:KEYS]).then_inc(done, 1)
                elif kind[0] == "q":
                    split_lo(qp[1][:, kind[1], :], p[:], qp[0][:, kind[1], :], UNSCALE).then_inc(done, 1)
                elif kind[0] == "U":
                    split_lo(uT[1][:], p[:].rearrange("p (t q) -> p t q", t=DT), uT[0][:]).then_inc(done, 1)
                else:
                    for i in range(2):
                        s = slice(64 * i, 64 * i + 64)
                        o = bass.ds(b * NQ, NQ)
                        last = split_lo(oT[1][s, kind[1], o], p[s, 64 * i:64 * i + 64], oT[0][s, kind[1], o], UNSCALE)
                    last.then_inc(done, 1)

            def chunk_max(t, c, b):
                dve.wait_ge(s_sim, CHUNKS * (HQ_TILES * b + t) + c + 1)
                dve.tensor_copy(spare[:, 1 + CHUNKS * t + c:2 + CHUNKS * t + c], psim[c][:, 0:1])
                m = LAST_MEDIA if c == CHUNKS - 1 else CH
                lo = c * CH
                ins = dve.tensor_tensor_reduce(probs[t % 2][:, lo:lo + m], psim[c][:, 0:m], mask_f[:, lo:lo + m], SCALE, LOWEST,
                                               ALU.add, ALU.max, cmax[:, t % 2, c:c + 1])
                if c == CHUNKS - 1:
                    ins = dve.tensor_scalar(probs[t % 2][:, F:KEYS], psim[c][:, m:m + NQ], SCALE, LOWEST, ALU.mult, ALU.max,
                                            accum_out=cmax[:, t % 2, 4:5])
                ins.then_inc(s_sfree, 1)

            def row_max(t, b):
                n = 4 * (HQ_TILES * b + t)
                c, m = cmax[:, t % 2, :], rmax[:, t % 2, :]
                dve.wait_ge(s_sfree, CHUNKS * (HQ_TILES * b + t) + CHUNKS)
                dve.tensor_reduce(m[:, 0:1], c[:, 0:4], AX.X, ALU.max).then_inc(s_rm, 1)
                dve.wait_ge(s_rm, n + 1)
                dve.scalar_tensor_tensor(m[:, 1:2], m[:, 0:1], qb_now[:, t:t + 1], c[:, 4:5], ALU.add, ALU.max).then_inc(s_rm, 1)
                dve.wait_ge(s_rm, n + 2)
                dve.tensor_scalar(m[:, 2:3], m[:, 1:2], -1.0, None, ALU.mult).then_inc(s_rm, 1)
                dve.tensor_tensor(m[:, 3:4], qb_now[:, t:t + 1], m[:, 1:2], ALU.subtract).then_inc(s_rm, 1)

            def attended(t, b):
                n = 6 * (HQ_TILES * b + t)
                s = rsum[:, t % 2, :]
                dve.tensor_tensor(unorm[:, 0:1], s[:, 0:1], s[:, 1:2], ALU.add).then_inc(s_u, 1)
                dve.wait_ge(s_u, n + 1)
                dve.reciprocal(unorm[:, 1:2], unorm[:, 0:1]).then_inc(s_u, 1)
                dve.wait_ge(s_u, n + 2)
                dve.tensor_tensor(unorm[:, 2:3], unorm[:, 1:2], s[:, 0:1], ALU.mult).then_inc(s_u, 1)
                dve.wait_ge(s_pv, HQ_TILES * b + t + 1)
                dve.scalar_tensor_tensor(usb[:, 0, :], media_bank(t)[:], unorm[:, 1:2], gm_bc[:], ALU.mult, ALU.mult).then_inc(s_u, 1)
                dve.wait_ge(s_u, n + 4)
                dve.scalar_tensor_tensor(usb[:, 1, :], bm_bc[:], unorm[:, 2:3], usb[:, 0, :], ALU.mult, ALU.add).then_inc(s_u, 1)
                dve.wait_ge(s_u, n + 5)
                dve.scalar_tensor_tensor(usb[:, 0, :], pul[:], unorm[:, 1:2], usb[:, 1, :], ALU.mult, ALU.add).then_inc(s_u, 1)

            def row_low(tiles, b):
                for k in tiles:
                    dve.wait_ge(s_nh, KT * b + k + 1)
                    if k < LAT:
                        dve.tensor_tensor(xn[1][:, k, :], xs[:, k, :], xn[0][:, k, :], ALU.subtract).then_inc(s_nl, 1)
                    else:
                        dve.tensor_tensor(xn[0][NQ:P, k, :], xs[NQ:P, k, :], xn[1][NQ:P, k, :], ALU.subtract).then_inc(s_nl, 1)

            def normalise(tiles, n):
                dve.wait_ge(s_rd, n)
                for k in tiles:
                    dve.tensor_scalar(xs[:, k, :], xs[:, k, :], mv[:, k, 0:1], rstd[:, k:k + 1],
                                      ALU.subtract, ALU.mult).then_inc(s_norm, 1)

            weight_low(1, wqs, wq_f)
            for dt in range(DT):
                dve.wait_ge(s_lhi, dt + 1)
                split_lo(latT[1][:, dt, :], psim[dt][:], latT[0][:, dt, :]).then_inc(s_llo, 1)
            media_stats(1, range(MT))
            def query_low(t):
                dve.wait_ge(s_qhi, t + 1)
                for i in range(2):
                    s = slice(64 * i, 64 * i + 64)
                    src = [*ptp, pum, pul][t][s, :].rearrange("p (b n) -> p b n", n=NQ)
                    last = split_lo(qbd[1][s, :, t, s], src, qbd[0][s, :, t, s], UNSCALE)
                last.then_inc(s_qlo, 1)

            query_low(0)
            dve.wait_ge(s_rd, 1)
            dve.scalar_tensor_tensor(shift[:], mv[:, :, 0], -1.0, rstd[:], ALU.mult, ALU.mult).then_inc(s_shift, 1)
            for t in range(1, HQ_TILES):
                query_low(t)
            dve.wait_ge(s_kvst, 16)
            for r in PREP[:XROUNDS]:
                take(r, 0)
                if r == PREP[3]:
                    weight_low(2, wk, wk_f)
                    normalise(range(ACT_TILES, MT), 1)
            dve.wait_ge(s_qlo, HQ_TILES)
            queries(0)
            for r in PREP[XROUNDS:]:
                take(r, 0)
            for t in range(DT):
                last = dve.tensor_tensor_reduce(usb[:, t % 2, :], wk_f[:, t, :], bm_bc[:], 1.0, 0.0, ALU.mult, ALU.add, bk[:, t:t + 1])
                last.then_inc(s_bt, 1)
                dve.wait_ge(s_bt, t + 1)
            dve.tensor_copy(bkh[0][:], bk[:]).then_inc(s_bt, 1)
            dve.wait_ge(s_bt, DT + 1)
            dve.tensor_tensor(bkh[1][:], bk[:], bkh[0][:], ALU.subtract).then_inc(s_bk, 1)

            def sums_with_beta(b):
                dve.tensor_copy(qb_now[:], qb_all[:, bass.ds(b * HQ_TILES, HQ_TILES)]).then_inc(s_qbn, 1)

            def batch(b, first, last):
                if not first:
                    attended(3, b - 1)
                if not first:
                    sums_with_beta(b)
                dve.wait_ge(s_mf, b + 1)
                for c in range(CHUNKS):
                    if first and c == CHUNKS - 1:
                        dve.wait_ge(s_qb, 1)
                        dve.tensor_scalar(qb_all[:], psim[3][:, 0:B * HQ_TILES], SCALE, None, ALU.mult).then_inc(s_qbs, 1)
                        dve.wait_ge(s_qbs, 1)
                        sums_with_beta(0)
                    chunk_max(0, c, b)
                    if c < 3:
                        row_low(range(3 * c, 3 * c + 3), b)
                dve.wait_ge(s_qbn, b + 1)
                row_max(0, b)
                row_low(range(9, 11), b)
                if not first:
                    rnd[0] = ROUNDS - 2
                    take(("U", 3), b - 1)
                row_low(range(11, KT), b)
                if first:
                    weight_low(3, wvs, wv_f)
                chunk_max(1, 0, b)
                chunk_max(1, 1, b)
                if not first:
                    take(("V", 3), b - 1)
                rnd[0] = 0
                chunk_max(1, 2, b)
                take(("P", 0, 0), b)
                chunk_max(1, 3, b)
                take(("P", 0, 1), b)
                row_max(1, b)
                for r in cells(0, last):
                    take(r, b)
                if not last:
                    media_stats(b + 2, range(0, 3))
                else:
                    dve.wait_ge(s_woh, 2)
                    for dt in range(DT):
                        split_lo(wo[1][:, dt, :], wo_f[:, dt, :], wo[0][:, dt, :], WEIGHT_SCALE)
                    split_lo(gw[1][:], gw_f[:], gw[0][:], WEIGHT_SCALE).then_inc(s_wol, 1)
                attended(0, b)
                for c in range(CHUNKS):
                    chunk_max(2, c, b)
                    if c > 1:
                        take(("P", 1, c - 2), b)
                row_max(2, b)
                if not last:
                    media_stats(b + 2, range(3, 5))
                for i, r in enumerate(cells(1, last)):
                    take(r, b)
                    if not last:
                        media_stats(b + 2, STATS_AFTER[i])
                attended(1, b)
                for c in range(CHUNKS):
                    chunk_max(3, c, b)
                    if not last and c < 2:
                        normalise(range(2 * c, 2 * c + 2), b + 2)
                    if c > 1:
                        take(("P", 2, c - 2), b)
                row_max(3, b)
                if not last:
                    queries(b + 1)
                for r in cells(2, last):
                    take(r, b + 1 if r[0] in "xq" else b)
                    if r in NORMALISED_AFTER and not last:
                        normalise(NORMALISED_AFTER[r], b + 2)
                attended(2, b)
                for r in cells(3, last):
                    take(r, b + 1 if r[0] in "xq" else b)

            STATS_AFTER = [range(5, 5), range(5, 8), range(8, 11), range(11, MT)]
            NORMALISED_AFTER = {("P", 2, 2): range(4, 6), ("x", 0): range(6, 8), ("x", 2): range(8, 10), ("P", 2, 3): range(10, 12),
                                ("V", 1): range(12, MT)}
            batch(0, True, False)
            with dve.Fori(1, B - 1) as b:
                batch(b, False, False)
            batch(B - 1, False, True)
            attended(3, B - 1)
            take(("U", 3), B - 1)
            take(("V", 3), B - 1)

        @block.tensor
        def _(pe):
            def product(out_, lhs, rhs, first, last):
                pe.matmul(out_, lhs[0], rhs[0], start=first, stop=False)
                pe.matmul(out_, lhs[0], rhs[1], start=False, stop=False)
                return pe.matmul(out_, lhs[1], rhs[0], start=False, stop=last)

            pe.wait_ge(s_id, 2)
            pe.wait_ge(s_lat, TT)
            for dt in range(DT):
                for t in range(TT):
                    last = pe.transpose(psim[dt][:, t * P:(t + 1) * P], lat[:, t, dt * P:(dt + 1) * P], ident[:])
                last.then_inc(s_ltp, 1)
            pe.wait_ge(s_wlo, 1)
            pe.wait_ge(s_llo, DT)
            for t in range(HQ_TILES):
                for dt in range(DT):
                    last = product([*ptp, pum, pul][t][:], [w[:, dt, t * P:(t + 1) * P] for w in wqs],
                                   [l[:, dt, :] for l in latT], dt == 0, dt == DT - 1)
                last.then_inc(s_qp, 1)
            rnd = [0]

            u_round = {}

            def normalised(b, tiles):
                if isinstance(b, int) and b == 0 and tiles <= ACT_TILES:
                    pe.wait_ge(s_norm0, tiles)
                else:
                    pe.wait_ge(s_norm, MT * b + tiles - ACT_TILES)

            def give(kind, b):
                if kind[0] in "xq":
                    r = PREP.index(kind)
                    p, done = psim[r % 3], s_xp
                    if r >= 3:
                        pe.wait_ge(s_xfree, NPREP * b + r - 2)
                    elif not (isinstance(b, int) and b == 0):
                        pe.wait_ge(s_sfree, CHUNKS * (HQ_TILES * b - 1) + r + 1)
                else:
                    r = rnd[0]
                    rnd[0] += 1
                    p, done = ptp[r % 2], s_tp
                    if not (isinstance(b, int) and b == 0 and r < 2):
                        pe.wait_ge(s_tfree, ROUNDS * b + r - 1)
                if kind[0] == "P":
                    t, g = kind[1], kind[2]
                    if g == 0:
                        pe.wait_ge(s_exp, HQ_TILES * b + t + 1)
                    tiles = range(4 * g, 4 * g + 4) if g < 3 else (FULL, LAT)
                    for i, k in enumerate(tiles):
                        n = rows(k) if k < LAT else P
                        c = k * P if k < LAT else F
                        last = pe.transpose(p[0:n, i * P:(i + 1) * P], probs[t % 2][:, c:c + n], ident[:])
                elif kind[0] == "x":
                    i = kind[1]
                    if i < 12:
                        if i % 4 == 0:
                            normalised(b, 4 * (i // 4) + 4)
                        for j in range(4):
                            last = pe.transpose(p[:, j * P:(j + 1) * P], xs[:, (i // 4) * 4 + j, (i % 4) * P:(i % 4 + 1) * P], ident[:])
                    else:
                        k, n = (FULL, REM) if i == 12 else (LAT, P)
                        if k == FULL:
                            normalised(b, MT)
                        else:
                            pe.wait_ge(s_ctx, 64 * (b + 1))
                        for dt in range(DT):
                            last = pe.transpose(p[:, dt * n:(dt + 1) * n], xs[0:n, k, dt * P:(dt + 1) * P], ident[0:n, 0:n])
                elif kind[0] == "q":
                    dt = kind[1]
                    pe.wait_ge(s_qn, b + 1)
                    if isinstance(b, int) and b == 0:
                        pe.wait_ge(s_wlo, 2)
                    for t in range(HQ_TILES):
                        last = product(p[:, t * P:(t + 1) * P], [w[:, t, dt * P:(dt + 1) * P] for w in wk], [q[:, t, :] for q in qnow], True, True)
                elif kind[0] == "U":
                    u_round[kind[1]] = r
                    pe.wait_ge(s_u, 6 * (HQ_TILES * b + kind[1]) + 6)
                    for dt in range(DT):
                        last = pe.transpose(p[:, dt * P:(dt + 1) * P], usb[:, 0, dt * P:(dt + 1) * P], ident[:])
                else:
                    t = kind[1]
                    if isinstance(b, int) and b == 0 and t == 0:
                        pe.wait_ge(s_wlo, 3)
                    pe.wait_ge(s_tfree, ROUNDS * b + u_round[t] + 1)
                    for dt in range(DT):
                        last = product(p[:, 0:P], [w[:, dt, t * P:(t + 1) * P] for w in wvs], [u[:, dt, :] for u in uT], dt == 0, dt == DT - 1)
                last.then_inc(done, 1)
                return r

            def scores(t, c, b):
                if t > 0:
                    pe.wait_ge(s_sfree, CHUNKS * (HQ_TILES * b + t - 1) + c + 1)
                elif c == CHUNKS - 1 and isinstance(b, int) and b == 0:
                    pe.wait_ge(s_qbs, 1)
                elif c == CHUNKS - 1:
                    pe.wait_ge(s_u, 6 * HQ_TILES * b - 2)
                n = LAST if c == CHUNKS - 1 else CH
                for dt in range(DT):
                    last = product(psim[c][:, 0:n], [q[:, dt, t * P:(t + 1) * P] for q in qp],
                                   [v[:, dt, c * CH:c * CH + n] for v in xT], dt == 0, dt == DT - 1)
                last.then_inc(s_sim, 1)

            def attend(t, k, b):
                if k == 0:
                    if t == HQ_TILES - 1:
                        pe.wait_ge(s_sfree, CHUNKS * (HQ_TILES * b + t) + CHUNKS)
                    elif not (isinstance(b, int) and b == 0 and t == 0):
                        pe.wait_ge(s_u, 6 * (HQ_TILES * b + t) - 2)
                    if t == 0:
                        pe.wait_ge(s_nl, KT * (b + 1))
                if k == LAT and not (isinstance(b, int) and b == 0 and t == 0):
                    pe.wait_ge(s_u, 6 * (HQ_TILES * b + t))
                if k % 4 == 0:
                    pe.wait_ge(s_tfree, ROUNDS * b + p_rounds[t][k // 4] + 1)
                if k < LAT:
                    n = rows(k)
                    product(media_bank(t)[:], [q[0:n, k, :] for q in pT[t % 2]], [v[0:n, k, :] for v in xn], k == 0, k == FULL)
                else:
                    pe.matmul(pul[:], pT[t % 2][0][:, k, :], xn[0][:, k, :], start=True, stop=False)
                    pe.matmul(pul[:], pT[t % 2][1][0:NQ, k, :], xn[0][0:NQ, k, :], start=False, stop=True).then_inc(s_pv, 1)

            for r in PREP:
                give(r, 0)

            def products_with_beta():
                pe.wait_ge(s_bk, 1)
                pe.wait_ge(s_qlo, HQ_TILES)
                for b in range(B):
                    for t in range(HQ_TILES):
                        n = b * HQ_TILES + t
                        last = product(psim[3][:, n:n + 1], [q[:, b, t, :] for q in qbd], [v[:, t:t + 1] for v in bkh], True, True)
                last.then_inc(s_qb, 1)

            def batch(b, first, last):
                def attend_all(t):
                    for k in range(KT):
                        attend(t, k, b)
                        for r in cells(t, last, [k]):
                            n = give(r, b + 1 if r[0] in "xq" else b)
                            if r[0] == "P":
                                p_rounds[r[1]].append(n)

                pe.wait_ge(s_xfree, NPREP * (b + 1))
                for c in range(CHUNKS):
                    if first and c == CHUNKS - 1:
                        products_with_beta()
                    scores(0, c, b)
                if not first:
                    rnd[0] = ROUNDS - 2
                    give(("U", 3), b - 1)
                for c in range(CHUNKS):
                    scores(1, c, b)
                    if c == 1:
                        if not first:
                            give(("V", 3), b - 1)
                        rnd[0] = 0
                        for q in p_rounds:
                            q.clear()
                    if c > 1:
                        p_rounds[0].append(give(("P", 0, c - 2), b))
                attend_all(0)
                for t in (1, 2):
                    for c in range(CHUNKS):
                        scores(t + 1, c, b)
                        if c > 1:
                            p_rounds[t].append(give(("P", t, c - 2), b))
                    attend_all(t)
                attend_all(3)

            p_rounds = [[], [], [], []]
            batch(0, True, False)
            with pe.Fori(1, B - 1) as b:
                batch(b, False, False)
            batch(B - 1, False, True)
            give(("U", 3), B - 1)
            give(("V", 3), B - 1)

        first_half.close()
        second_half(nc, es, xres, oT, ident, wo, gw, s_wol, w1, w2, out)


def second_half(nc, es, xres, oT, ident, wo, gw, s_wol, w1, w2, out):
    TT, D = xres.shape[1], xres.shape[2]
    DT = D // P
    TOK = TT * P
    NQ = P // 2
    NSETS, NJ, _, _, HC = w1.shape
    HT = HC // P
    E = gw[0].shape[2]
    assert NJ == 4 and NSETS == E + 1 and E % 2 == 0 and TOK % P == 0

    def sb(name, shape, dt):
        return es.enter_context(nc.sbuf_tensor(name, shape, dt))

    def sem(name):
        return es.enter_context(nc.semaphore(name))

    CHUNK = 4 * HC
    PARITY = NJ * 2 * 2 * CHUNK
    wbuf = sb("weights_split", [P, 2 * PARITY], F16)

    def split_weights(parity, j, k):
        at = [(((parity * NJ + j) * 2 + k) * 2 + h) * CHUNK for h in range(2)]
        return [wbuf[:, a:a + CHUNK].rearrange("p (t c) -> p t c", t=4) for a in at]

    place = [PARITY]

    def early(words, dt, parts):
        n = words * (2 if dt == F32 else 1)
        a = wbuf[:, place[0]:place[0] + n]
        place[0] += n
        return (a.bitcast(F32) if dt == F32 else a).rearrange("p (t c) -> p t c", t=parts)

    x1 = early(TT * D, F32, TT)
    x2n = early(TT * D, F32, TT)
    x2T = early(TT * D, F32, TT).rearrange("p t (d q) -> p t d q", d=DT)
    x3n = early(TT * D, F32, TT)
    pbd = early(TT * P, F32, TT)
    assert place[0] <= 2 * PARITY
    place[0] = PARITY // 2
    x3T = [early(DT * TOK, F16, DT) for _ in range(2)]
    hT = [[early(HT * TOK, F16, HT) for _ in range(2)] for _ in range(2)]
    hf = early(2 * TOK, F32, 2)
    assert place[0] <= PARITY

    x2 = xres
    x3r = oT
    stats = sb("stats2", [P, TT, 6], F32)
    mv = sb("mean_var2", [P, TT, 2], F32)
    rstd = sb("rstd2", [P, TT], F32)
    half = sb("minus_half2", [P, TT], F32)
    smax = sb("self_max", [P, TT], F32)
    ssum = sb("self_sum", [P, TT], F32)
    srec = sb("self_rec", [P, TT], F32)
    iota = sb("iota", [P, P], F32)
    block_start = sb("block_start", [P, TT], F32)
    slot_now = sb("slot_now", [P, TT], F32)
    ident16 = sb("ident_f16", [P, P], F16)
    before_f = sb("before_f32", [P, P], F32)
    before = sb("before", [P, P], F16)
    ones = sb("ones", [P, P], F16)
    logits = sb("gate_logits", [P, TT, E], F32)
    top = sb("top_values", [P, TT, 8], F32)
    topi = sb("top_index", [P, TT, 8], U32)
    topf = sb("top_index_f", [P, TT, 2], F32)
    gate = sb("gate_step", [P, TT, 4], F32)
    hot = [sb("first_choice", [P, TT, E], F32), sb("second_choice", [P, TT, E], F32)]
    chosen = sb("chosen", [P, TT, E], F32)
    chosen16 = sb("chosen_f16", [P, TT, E], F16)
    gates = sb("gates", [P, TT, E], F32)
    first_gate = sb("first_gate", [P, TT, E], F32)
    gsplit = sb("gates_split", [P, TT, E, 2], F16)
    slot = sb("slot", [P, TT, E], F32)
    rank1 = sb("rank_step", [P, TT, E], F32)
    PAD = 4
    run = sb("block_sums", [1, 4, PAD + E], F32)
    table = sb("counts", [1, E + E + 1], I32)
    wst = [[sb(f"w{k + 1}_f32_{i}", [P, 4, HC], F32) for i in range(2)] for k in range(2)]
    sel = sb("selection", [P, TT, P], F16)
    selT = sb("selection_t", [P, TOK], F16)
    gnow = sb("gates_now", [P, TT, 2], F16)
    spare = sb("pool_spare2", [P, 1], F32)
    gslot = sb("slot_gate", [P, 1], F32)
    xb = [sb("block_x_hi", [P, DT, P], F16), sb("block_x_lo", [P, DT, P], F16)]
    bf = sb("block_hidden_f32", [P, 2, HC], F32)
    bT = [sb("block_hidden_hi", [P, NJ, HC], F16), sb("block_hidden_lo", [P, NJ, HC], F16)]
    yb = [sb("block_y_hi", [P, D], F16), sb("block_y_lo", [P, D], F16)]
    pb = [es.enter_context(nc.psum_tensor(f"p_bank{i}", [P, 512], F32)) for i in range(8)]
    p_y, p_t = pb[6], pb[7]
    p_selT = p_t[:, 0:256].bitcast(F16)
    p_gate = p_t[:, 256:257]

    s_y, s_x1 = sem("out_projected"), sem("x1_ready")
    s_half, s_zero, s_iota = sem("minus_half2_ready"), sem("self_probs_zeroed"), sem("iota_ready")
    s_before, s_const = sem("before_ready"), sem("constants_f16")
    s_st, s_rs, s_n2 = sem("norm_stats"), sem("norm_rstd"), sem("self_norm_ready")
    s_t2, s_c2 = sem("self_transposed"), sem("self_t_ready")
    s_ss, s_mx, s_ex, s_pn = sem("self_scores"), sem("self_max_ready"), sem("self_exp"), sem("self_probs_ready")
    s_so, s_x2, s_n3 = sem("self_out"), sem("x_after_self_ready"), sem("ffn_norm_ready")
    s_t3, s_h3, s_l3 = sem("ffn_transposed"), sem("ffn_t_hi"), sem("ffn_t_lo")
    s_r3h, s_r3l = sem("ffn_rows_hi"), sem("ffn_rows_lo")
    s_lg, s_gt, s_ge = sem("gate_logits_product"), sem("gate_step_done"), sem("gate_exp")
    s_rk, s_rt = sem("ranks_product"), sem("routing_step")
    s_cnt = sem("counts_ready")
    s_wl = [[sem(f"w{k + 1}_loaded{i}") for i in range(2)] for k in range(2)]
    s_wh = [sem(f"w{k + 1}_hi_ready") for k in range(2)]
    s_wlo = [sem(f"w{k + 1}_lo_ready") for k in range(2)]
    s_h, s_hf, s_hh, s_hl = sem("hidden_product"), sem("hidden_ready"), sem("hidden_hi"), sem("hidden_lo")
    s_yp = sem("shared_product")
    s_out = sem("stored")
    s_rc = sem("self_reciprocal")
    s_g1, s_g2, s_g3, s_g4, s_g5 = (sem(f"gate_{n}") for n in ("logits", "top", "index", "weights", "onehot"))
    s_sel, s_gp, s_tr, s_sc = sem("selection_ready"), sem("block_gathered"), sem("selection_transposed"), sem("block_scattered")
    s_sn = sem("slot_now_ready")
    s_xh, s_xl = sem("block_x_hi_ready"), sem("block_x_lo_ready")
    s_stc, s_gs = sem("selection_t_ready"), sem("slot_gate_ready")
    s_bh, s_bf, s_bhh, s_bl = sem("block_hidden_product"), sem("block_hidden_ready"), sem("block_hidden_hi_ready"), sem("block_hidden_lo_ready")
    s_by, s_yh, s_yl = sem("block_product"), sem("block_y_hi_ready"), sem("block_y_lo_ready")
    s_ye = sem("ffn_added")

    def all_blocks(eng, block):
        eng.wait_ge(s_cnt, 1)

        def expert(e, parity, last):
            es_ = slice(e, e + 1) if isinstance(e, int) else bass.ds(e, 1)
            eo_ = slice(E + e, E + e + 1) if isinstance(e, int) else bass.ds(E + e, 1)
            count = eng.value_load(table[0:1, es_], min_val=0, max_val=TOK)
            n0 = eng.value_load(table[0:1, eo_], min_val=0, max_val=2 * TOK // P + E)
            block(e, 0, n0, parity, not last)
            with eng.If(count > P):
                with eng.Fori(1, TOK // P) as k:
                    with eng.If(count > k * P):
                        block(e, k, n0 + k, parity, False)

        with eng.Fori(0, E // 2 - 1) as pair:
            expert(pair * 2, 1, False)
            expert(pair * 2 + 1, 0, False)
        expert(E - 2, 1, False)
        expert(E - 1, 0, True)
        return eng.value_load(table[0:1, 2 * E:2 * E + 1], min_val=E, max_val=2 * TOK // P + E)

    block = es.enter_context(nc.Block())

    @block.sync
    def _(sp):
        def load(s, j, first):
            sets = slice(s, s + 1) if isinstance(s, int) else bass.ds(s, 1)
            for k, w in enumerate((w1, w2)):
                if not first:
                    sp.wait_ge(s_wh[k], NJ * s + j - 1)
                    sp.wait_ge(s_wlo[k], NJ * s + j - 1)
                sp.dma_start(wst[k][j % 2][:], w[sets, j].rearrange("o p t h -> p (o t) h")).then_inc(s_wl[k][j % 2], 16)

        for j in range(NJ):
            load(0, j, j < 2)
        with sp.Fori(1, NSETS) as s:
            for j in range(NJ):
                load(s, j, False)
        for i in range(TT):
            sp.wait_ge(s_ye, i + 1)
            sp.dma_start(out.rearrange("b n d -> (b n) d")[i * P:(i + 1) * P, :], x2[:, i, :]).then_inc(s_out, 16)
        sp.wait_ge(s_out, 16 * TT)

    @block.gpsimd
    def _(pool):
        pool.memset(half[:], -0.5).then_inc(s_half, 1)
        pool.memset(before_f[:], 1.0).then_inc(s_half, 1)
        pool.iota(iota[:], [[1, P]], base=0, channel_multiplier=0, allow_small_or_imprecise_dtypes=True).then_inc(s_iota, 1)
        pool.iota(block_start[:], [[P, TT]], base=0, channel_multiplier=0, allow_small_or_imprecise_dtypes=True).then_inc(s_iota, 1)
        pool.wait_ge(s_half, 2)
        pool.affine_select(out=before_f[:], in_=before_f[:], compare_op=ALU.is_gt, fill=0.0, base=0,
                           pattern=[[1, P]], channel_multiplier=-1).then_inc(s_before, 1)
        for n in range(2):
            pool.wait_ge(s_st, 3 * (n + 1))
            pool.tensor_tensor(rstd[:], mv[:, :, 1], half[:], ALU.pow).then_inc(s_rs, 1)

        def block_(e, k, n, parity, prefetch):
            experts = slice(e, e + 1) if isinstance(e, int) else bass.ds(e, 1)
            ks = slice(k, k + 1) if isinstance(k, int) else bass.ds(k, 1)
            pool.wait_ge(s_tr, n + 1)
            pool.tensor_tensor(spare[:], half[:, 0:1], half[:, 0:1], ALU.add)
            pool.tensor_tensor(slot_now[:], slot[:, :, experts].rearrange("p t o -> p (t o)"),
                               block_start[:, ks].broadcast_to((P, TT)), ALU.subtract).then_inc(s_sn, 1)
            pool.wait_ge(s_sn, n + 1)
            pool.tensor_tensor(spare[:], half[:, 0:1], half[:, 0:1], ALU.add)
            pool.tensor_copy(gnow[:], gsplit[:, :, experts, :].rearrange("p t o h -> p t (o h)"))
            for i in range(TT):
                last = pool.tensor_scalar(sel[:, i, :], iota[:, 0:P], slot_now[:, i:i + 1], None, ALU.is_equal)
            last.then_inc(s_sel, 1)

        pool.wait_ge(s_iota, 2)
        all_blocks(pool, block_)

    @block.scalar
    def _(act):
        def copy(out_, in_, scale=1.0):
            return act.activation(out_, in_, ACT.Copy, scale=scale)

        def high(s, j, k, parity, chunk, free=None):
            act.wait_ge(s_wl[k][j % 2], 16 * (NJ // 2 * s + j // 2 + 1))
            if free is not None:
                act.wait_ge(*free)
            copy(split_weights(parity, chunk, k)[0], wst[k][j % 2][:], WEIGHT_SCALE).then_inc(s_wh[k], 1)

        high(0, 0, 0, 0, 0)
        high(0, 0, 1, 0, 0)
        for i in range(TT):
            act.wait_ge(s_t2, i + 1)
            copy(x2T[:, i, :, :], pb[4 + i][:].rearrange("p (t q) -> p t q", q=P)).then_inc(s_c2, 1)
        act.wait_ge(s_zero, 1)
        for i in range(TT):
            act.wait_ge(s_mx, i + 1)
            for b in range(2):
                r = slice(NQ * b, NQ * b + NQ)
                last = act.activation(pbd[r, i, r], pb[i][r, r], ACT.Exp, bias=smax[r, i:i + 1], accum_out=ssum[r, i:i + 1])
            last.then_inc(s_ex, 1)
        high(0, 1, 0, 0, 1)
        high(0, 1, 1, 0, 1)
        for i in range(TT):
            act.wait_ge(s_t3, i + 1)
            copy(x3T[0][:, :, i * P:(i + 1) * P], pb[i][:].rearrange("p (t q) -> p t q", q=P)).then_inc(s_h3, 1)

        def hidden(j):
            for ht in range(HT):
                n = HT * j + ht
                act.wait_ge(s_h, n + 1)
                if n >= 2:
                    act.wait_ge(s_hl, n - 1)
                act.activation(hf[:, ht % 2, :], pb[4 + ht % 2][:], ACT.Silu, scale=UNSCALE).then_inc(s_hf, 1)

        act.wait_ge(s_n3, TT)
        hidden(0)
        hidden(1)
        high(0, 2, 0, 0, 0, (s_h, HT))
        for i in range(TT):
            copy(x3r[0][:, i, :], x3n[:, i, :]).then_inc(s_r3h, 1)
        act.wait_ge(s_gt, TT)
        act.activation(gate[:, :, 1], gate[:, :, 0], ACT.Exp).then_inc(s_ge, 1)
        high(0, 3, 0, 0, 1, (s_h, 2 * HT))
        high(0, 2, 1, 0, 0, (s_yp, TT))
        hidden(2)
        high(0, 3, 1, 0, 1, (s_yp, 2 * TT))
        high(1, 0, 0, 1, 0)
        high(1, 0, 1, 1, 0)
        hidden(3)
        for j in range(1, NJ):
            high(1, j, 0, 1, j)
            high(1, j, 1, 1, j)

        def y_high(n):
            act.wait_ge(s_by, n + 1)
            act.wait_ge(s_gs, n + 1)
            copy(yb[0][:], p_y[:], gslot[:, 0:1]).then_inc(s_yh, 1)

        def block_(e, k, n, parity, prefetch):
            def next_weights(*pieces):
                if prefetch:
                    for piece in pieces:
                        high(e + 2, piece // 2, piece % 2, 1 - parity, piece // 2)

            def silu(j):
                act.wait_ge(s_bh, n * NJ + (j + 1))
                if j >= 2:
                    act.wait_ge(s_bl, n * NJ + (j - 1))
                act.activation(bf[:, j % 2, :], pb[4 + j % 2][:], ACT.Silu, scale=UNSCALE).then_inc(s_bf, 1)
                act.wait_ge(s_bf, n * NJ + (j + 1))
                copy(bT[0][:, j, :], bf[:, j % 2, :]).then_inc(s_bhh, 1)

            y_high(n)
            act.wait_ge(s_gp, n * 2 + 1)
            copy(xb[0][:], pb[4][:].rearrange("p (t q) -> p t q", q=P)).then_inc(s_xh, 1)
            next_weights(0)
            act.wait_ge(s_gs, n + 2)
            act.wait_ge(s_sc, n + 1)
            copy(selT[:], p_selT).then_inc(s_stc, 1)
            next_weights(1)
            silu(0)
            next_weights(2)
            silu(1)
            next_weights(3, 4)
            silu(2)
            next_weights(5, 6)
            silu(3)
            next_weights(7)

        total = all_blocks(act, block_)
        y_high(total)

    @block.vector
    def _(dve):
        def low(s, j, k, parity, chunk):
            hi, lo = split_weights(parity, chunk, k)
            dve.wait_ge(s_wh[k], NJ * s + j + 1)
            for t in range(4):
                last = dve.scalar_tensor_tensor(lo[:, t, :], wst[k][j % 2][:, t, :], WEIGHT_SCALE, hi[:, t, :], ALU.mult, ALU.subtract)
            last.then_inc(s_wlo[k], 1)

        dve.memset(pbd, 0.0).then_inc(s_zero, 1)
        dve.memset(ones[:], 1.0)
        dve.tensor_copy(ident16[:], ident[:])
        dve.memset(gslot[:], 0.0).then_inc(s_gs, 1)
        dve.memset(selT[:], 0.0)
        dve.memset(run[:], 0.0)
        dve.memset(table[:], 0)
        dve.wait_ge(s_before, 1)
        dve.tensor_copy(before[:], before_f[:]).then_inc(s_const, 1)

        def layernorm(src, dst, ready, n, done, make):
            for i in range(TT):
                make(i)
                dve.wait_ge(ready, i + 1)
                last = dve.bn_stats(stats[:, i, :], src[:, i, :])
            last.then_inc(s_st, 1)
            dve.wait_ge(s_st, 3 * n + 1)
            for i in range(TT):
                last = dve.bn_aggr(mv[:, i, :], stats[:, i, :])
            last.then_inc(s_st, 1)
            dve.wait_ge(s_st, 3 * n + 2)
            dve.tensor_scalar(mv[:, :, 1], mv[:, :, 1], EPS, None, ALU.add).then_inc(s_st, 1)
            dve.wait_ge(s_rs, n + 1)
            for i in range(TT):
                dve.tensor_scalar(dst[:, i, :], src[:, i, :], mv[:, i, 0:1], rstd[:, i:i + 1],
                                  ALU.subtract, ALU.mult).then_inc(done, 1)

        def add_projected(i):
            dve.wait_ge(s_y, i + 1)
            dve.scalar_tensor_tensor(x1[:, i, :], pb[i][:], UNSCALE, xres[:, i, :], ALU.mult, ALU.add).then_inc(s_x1, 1)

        def add_attended(i):
            dve.wait_ge(s_so, i + 1)
            dve.tensor_tensor(x2[:, i, :], pb[4 + i][:], x1[:, i, :], ALU.add).then_inc(s_x2, 1)

        layernorm(x1, x2n, s_x1, 0, s_n2, add_projected)
        low(0, 0, 0, 0, 0)
        for i in range(TT):
            dve.wait_ge(s_ss, i + 1)
            for b in range(2):
                r = slice(NQ * b, NQ * b + NQ)
                last = dve.tensor_reduce(smax[r, i:i + 1], pb[i][r, r], AX.X, ALU.max, negate=True)
            last.then_inc(s_mx, 1)
        for i in range(TT):
            dve.wait_ge(s_ex, i + 1)
            dve.reciprocal(srec[:, i:i + 1], ssum[:, i:i + 1]).then_inc(s_rc, 1)
            dve.wait_ge(s_rc, i + 1)
            dve.tensor_scalar(pbd[:, i, :], pbd[:, i, :], srec[:, i:i + 1], None, ALU.mult).then_inc(s_pn, 1)
        layernorm(x2, x3n, s_x2, 1, s_n3, add_attended)
        for i in range(TT):
            c = slice(i * P, (i + 1) * P)
            dve.wait_ge(s_h3, i + 1)
            dve.tensor_tensor(x3T[1][:, :, c], pb[i][:].rearrange("p (t q) -> p t q", q=P), x3T[0][:, :, c], ALU.subtract).then_inc(s_l3, 1)

        def hidden(j):
            for ht in range(HT):
                n = HT * j + ht
                dve.wait_ge(s_hf, n + 1)
                if j >= 2:
                    dve.wait_ge(s_yp, TT * (j - 1))
                dve.tensor_copy(hT[j % 2][0][:, ht, :], hf[:, ht % 2, :]).then_inc(s_hh, 1)
                dve.wait_ge(s_hh, n + 1)
                dve.tensor_tensor(hT[j % 2][1][:, ht, :], hf[:, ht % 2, :], hT[j % 2][0][:, ht, :], ALU.subtract).then_inc(s_hl, 1)

        low(0, 1, 0, 0, 1)
        dve.wait_ge(s_lg, 1)
        dve.tensor_scalar(logits[:], p_y[:, 0:TT * E].rearrange("p (t e) -> p t e", e=E), UNSCALE, None, ALU.mult).then_inc(s_g1, 1)
        hidden(0)
        low(0, 0, 1, 0, 0)
        hidden(1)
        low(0, 2, 0, 0, 0)
        low(0, 1, 1, 0, 1)
        for i in range(TT):
            dve.wait_ge(s_g1, 1)
            dve.max(top[:, i, :], logits[:, i, :]).then_inc(s_g2, 1)
        for i in range(TT):
            dve.wait_ge(s_g2, i + 1)
            dve.max_index(topi[:, i, :], top[:, i, :], logits[:, i, :]).then_inc(s_g3, 1)
            dve.tensor_tensor(gate[:, i, 0:1], top[:, i, 1:2], top[:, i, 0:1], ALU.subtract).then_inc(s_gt, 1)
        dve.wait_ge(s_g3, TT)
        dve.tensor_copy(topf[:], topi[:, :, 0:2]).then_inc(s_g4, 1)
        dve.wait_ge(s_iota, 1)
        dve.wait_ge(s_g4, 1)
        for i in range(TT):
            for c in range(2):
                last = dve.tensor_scalar(hot[c][:, i, :], iota[:, 0:E], topf[:, i, c:c + 1], None, ALU.is_equal)
        last.then_inc(s_rt, 1)
        dve.wait_ge(s_rt, 1)
        dve.tensor_tensor(chosen[:], hot[0][:], hot[1][:], ALU.add).then_inc(s_rt, 1)
        dve.wait_ge(s_rt, 2)
        dve.tensor_copy(chosen16[:], chosen[:]).then_inc(s_rt, 1)
        for i in range(TT):
            dve.wait_ge(s_r3h, i + 1)
            dve.tensor_tensor(x3r[1][:, i, :], x3n[:, i, :], x3r[0][:, i, :], ALU.subtract).then_inc(s_r3l, 1)
        dve.wait_ge(s_ge, 1)
        dve.tensor_scalar(gate[:, :, 2], gate[:, :, 1], 1.0, None, ALU.add).then_inc(s_g4, 1)
        dve.wait_ge(s_g4, 2)
        dve.reciprocal(gate[:, :, 3], gate[:, :, 2]).then_inc(s_g4, 1)
        dve.wait_ge(s_g4, 3)
        dve.tensor_tensor(gate[:, :, 2], gate[:, :, 3], gate[:, :, 1], ALU.mult).then_inc(s_g4, 1)
        dve.wait_ge(s_g4, 4)
        for i in range(TT):
            last = dve.tensor_scalar(first_gate[:, i, :], hot[0][:, i, :], gate[:, i, 3:4], None, ALU.mult)
        last.then_inc(s_g5, 1)
        dve.wait_ge(s_g5, 1)
        for i in range(TT):
            last = dve.scalar_tensor_tensor(gates[:, i, :], hot[1][:, i, :], gate[:, i, 2:3], first_gate[:, i, :], ALU.mult, ALU.add)
        last.then_inc(s_g5, 1)
        dve.wait_ge(s_g5, 2)
        dve.tensor_copy(gsplit[:, :, :, 0], gates[:]).then_inc(s_g5, 1)
        dve.wait_ge(s_g5, 3)
        dve.tensor_tensor(gsplit[:, :, :, 1], gates[:], gsplit[:, :, :, 0], ALU.subtract).then_inc(s_g5, 1)
        low(0, 3, 0, 0, 1)
        low(0, 2, 1, 0, 0)
        hidden(2)
        dve.wait_ge(s_rk, 1)
        dve.scalar_tensor_tensor(rank1[:], p_t[:, 0:TT * E].rearrange("p (t e) -> p t e", e=E), 1.0, chosen[:], ALU.add, ALU.mult).then_inc(s_rt, 1)
        dve.wait_ge(s_rt, 4)
        dve.tensor_scalar(slot[:], rank1[:], -1.0, None, ALU.add).then_inc(s_rt, 1)
        counts = p_t[0:1, TT * E:(TT + 1) * E]
        dve.tensor_copy(table[0:1, 0:E], counts)
        dve.tensor_scalar(run[:, 3, PAD:], counts, P + 0.5, 1.0, ALU.is_gt, ALU.add).then_inc(s_rt, 1)
        for i, k in enumerate((2, 3)):
            dve.wait_ge(s_rt, 6 + i)
            dst = run[:, 2 if k == 2 else 0, PAD:]
            dve.scalar_tensor_tensor(dst, counts, k * P + 0.5, run[:, 3 if k == 2 else 2, PAD:], ALU.is_gt, ALU.add).then_inc(s_rt, 1)
        for i in range(3):
            a, b = i % 2, (i + 1) % 2
            dve.wait_ge(s_rt, 8 + i)
            dve.tensor_tensor(run[:, b, PAD:], run[:, a, PAD:], run[:, a, PAD - (1 << i):PAD + E - (1 << i)], ALU.add).then_inc(s_rt, 1)
        dve.wait_ge(s_rt, 11)
        dve.tensor_copy(table[0:1, E + 1:], run[:, 1, PAD:]).then_inc(s_cnt, 1)
        low(0, 3, 1, 0, 1)
        low(1, 0, 0, 1, 0)
        low(1, 0, 1, 1, 0)
        hidden(3)
        for j in range(1, NJ):
            low(1, j, 0, 1, j)
            low(1, j, 1, 1, j)

        def y_low(n):
            dve.wait_ge(s_yh, n + 1)
            dve.scalar_tensor_tensor(yb[1][:], p_y[:], gslot[:, 0:1], yb[0][:], ALU.mult, ALU.subtract).then_inc(s_yl, 1)

        def block_(e, k, n, parity, prefetch):
            def next_weights(*pieces):
                if prefetch:
                    for piece in pieces:
                        low(e + 2, piece // 2, piece % 2, 1 - parity, piece // 2)

            def hidden_low(j):
                dve.wait_ge(s_bhh, n * NJ + (j + 1))
                dve.tensor_tensor(bT[1][:, j, :], bf[:, j % 2, :], bT[0][:, j, :], ALU.subtract).then_inc(s_bl, 1)

            y_low(n)
            dve.wait_ge(s_xh, n + 1)
            dve.wait_ge(s_gp, n * 2 + 2)
            dve.tensor_copy(xb[1][:], pb[5][:].rearrange("p (t q) -> p t q", q=P)).then_inc(s_xl, 1)
            dve.wait_ge(s_tr, n + 2)
            dve.wait_ge(s_yl, n + 1)
            dve.tensor_copy(gslot[:], p_gate).then_inc(s_gs, 1)
            next_weights(0)
            next_weights(1)
            hidden_low(0)
            next_weights(2)
            hidden_low(1)
            next_weights(3, 4)
            hidden_low(2)
            next_weights(5)
            hidden_low(3)
            next_weights(6, 7)

        total = all_blocks(dve, block_)
        y_low(total)
        for i in range(TT):
            dve.wait_ge(s_yp, NJ * TT + i + 1)
            dve.scalar_tensor_tensor(x2[:, i, :], pb[i][:], UNSCALE, x2[:, i, :], ALU.mult, ALU.add).then_inc(s_ye, 1)

    @block.tensor
    def _(pe):
        def product(out_, lhs, rhs, first, last):
            pe.matmul(out_, lhs[0], rhs[0], start=first, stop=False)
            pe.matmul(out_, lhs[0], rhs[1], start=False, stop=False)
            return pe.matmul(out_, lhs[1], rhs[0], start=False, stop=last)

        pe.wait_ge(s_wol, 1)
        for i in range(TT):
            for t in range(DT):
                last = product(pb[i][:], [o[:, t, i * P:(i + 1) * P] for o in oT], [w[:, t, :] for w in wo], t == 0, t == DT - 1)
            last.then_inc(s_y, 1)
        for i in range(TT):
            pe.wait_ge(s_n2, i + 1)
            for dt in range(DT):
                last = pe.transpose(pb[4 + i][:, dt * P:(dt + 1) * P], x2n[:, i, dt * P:(dt + 1) * P], ident[:])
            last.then_inc(s_t2, 1)
        for i in range(TT):
            pe.wait_ge(s_c2, i + 1)
            pe.wait_ge(s_x1, i + 1)
            for dt in range(DT):
                last = pe.matmul(pb[i][:, 0:P], x2T[:, i, dt, :], x2T[:, i, dt, :], start=dt == 0, stop=dt == DT - 1)
            last.then_inc(s_ss, 1)
        for i in range(TT):
            pe.wait_ge(s_pn, i + 1)
            pe.matmul(pb[4 + i][:], pbd[:, i, :], x2n[:, i, :], start=True, stop=True).then_inc(s_so, 1)
        for i in range(TT):
            pe.wait_ge(s_n3, i + 1)
            for dt in range(DT):
                last = pe.transpose(pb[i][:, dt * P:(dt + 1) * P], x3n[:, i, dt * P:(dt + 1) * P], ident[:])
            last.then_inc(s_t3, 1)
        for i in range(TT):
            pe.wait_ge(s_l3, i + 1)
            for dt in range(DT):
                last = product(p_y[:, i * E:(i + 1) * E], [v[:, dt, i * P:(i + 1) * P] for v in x3T], [g[:, dt, :] for g in gw], dt == 0, dt == DT - 1)
        last.then_inc(s_lg, 1)

        def hidden(j):
            pe.wait_ge(s_wlo[0], j + 1)
            for ht in range(HT):
                n = HT * j + ht
                if n >= 2:
                    pe.wait_ge(s_hf, n - 1)
                w = split_weights(0, j % 2, 0)
                for dt in range(DT):
                    last = product(pb[4 + ht % 2][:], [v[:, dt, ht * P:(ht + 1) * P] for v in w], [v[:, dt, :] for v in x3T], dt == 0, dt == DT - 1)
                last.then_inc(s_h, 1)

        def output(j):
            pe.wait_ge(s_wlo[1], j + 1)
            pe.wait_ge(s_hl, HT * j + HT)
            w = split_weights(0, j % 2, 1)
            for i in range(TT):
                for ht in range(HT):
                    last = product(pb[i][:], [h[:, ht, i * P:(i + 1) * P] for h in hT[j % 2]], [v[:, ht, :] for v in w],
                                   j == 0 and ht == 0, False)
                last.then_inc(s_yp, 1)

        hidden(0)
        hidden(1)
        output(0)
        hidden(2)
        pe.wait_ge(s_const, 1)
        pe.wait_ge(s_rt, 3)
        for i in range(TT):
            for t in range(i):
                pe.matmul(p_t[:, i * E:(i + 1) * E], ones[:], chosen16[:, t, :], start=t == 0, stop=False)
            pe.matmul(p_t[:, i * E:(i + 1) * E], before[:], chosen16[:, i, :], start=i == 0, stop=True)
        for t in range(TT):
            last = pe.matmul(p_t[:, TT * E:(TT + 1) * E], ones[:], chosen16[:, t, :], start=t == 0, stop=t == TT - 1)
        last.then_inc(s_rk, 1)
        output(1)
        hidden(3)
        output(2)
        pe.wait_ge(s_g1, 1)
        pe.matmul(p_y[:], selT[:, 0:P], selT[:], start=True, stop=True).then_inc(s_by, 1)
        pe.wait_ge(s_cnt, 1)
        pe.matmul(p_gate, selT[:, 0:P], selT[:, 0:1], start=True, stop=True).then_inc(s_tr, 1)
        output(NJ - 1)

        def scatter(n, final):
            pe.wait_ge(s_yl, n + 1)
            for i in range(TT):
                for h in range(2):
                    last = pe.matmul(pb[i][:], selT[:, i * P:(i + 1) * P], yb[h][:], start=False, stop=final and h == 1)
                if final:
                    last.then_inc(s_yp, 1)
            if not final:
                last.then_inc(s_sc, 1)

        def block_(e, k, n, parity, prefetch):
            def b_hidden(j):
                if isinstance(k, int):
                    pe.wait_ge(s_wlo[0], (e + 1) * NJ + (j + 1))
                if j >= 2:
                    pe.wait_ge(s_bf, n * NJ + (j - 1))
                w = split_weights(parity, j, 0)
                for ht in range(HT):
                    for dt in range(DT):
                        last = product(pb[4 + j % 2][:, ht * P:(ht + 1) * P], [v[:, dt, ht * P:(ht + 1) * P] for v in w],
                                       [v[:, dt, :] for v in xb], dt == 0, dt == DT - 1)
                last.then_inc(s_bh, 1)

            def b_output(j):
                if isinstance(k, int):
                    pe.wait_ge(s_wlo[1], (e + 1) * NJ + (j + 1))
                pe.wait_ge(s_bl, n * NJ + (j + 1))
                w = split_weights(parity, j, 1)
                for ht in range(HT):
                    last = product(p_y[:], [v[:, j, ht * P:(ht + 1) * P] for v in bT], [v[:, ht, :] for v in w],
                                   j == 0 and ht == 0, j == NJ - 1 and ht == HT - 1)
                if j == NJ - 1:
                    last.then_inc(s_by, 1)

            pe.wait_ge(s_sel, n + 1)
            for h in range(2):
                for dt in range(DT):
                    for i in range(TT):
                        last = pe.matmul(pb[4 + h][:, dt * P:(dt + 1) * P], x3r[h][:, i, dt * P:(dt + 1) * P], sel[:, i, :],
                                         start=i == 0, stop=i == TT - 1)
                last.then_inc(s_gp, 1)
            for i in range(TT):
                pe.transpose(p_selT[:, i * P:(i + 1) * P], sel[:, i, :], ident16[:])
            for i in range(TT):
                for h in range(2):
                    last = pe.matmul(p_gate, sel[:, i, :], gnow[:, i, h:h + 1], start=i == 0 and h == 0, stop=i == TT - 1 and h == 1)
            last.then_inc(s_tr, 1)
            scatter(n, False)
            pe.wait_ge(s_xl, n + 1)
            b_hidden(0)
            for j in range(1, NJ):
                b_hidden(j)
                b_output(j - 1)
            b_output(NJ - 1)

        total = all_blocks(pe, block_)
        scatter(total, True)


def kernel(x, ctx_1024, mask_BxS2_bk0, L0_xattn_kv_gate, L0_xattn_gamma_media, L0_xattn_beta_media, L0_xattn_gamma_lat,
           L0_xattn_beta_lat, L0_xattn_Wq, L0_xattn_Wk, L0_xattn_Wv, L0_xattn_Wout, L0_ffn_shared_w1, L0_ffn_shared_w2,
           L0_ffn_experts_w1, L0_ffn_experts_w2, L0_ffn_gate_w):
    import numpy as np
    import concourse.bacc as bacc
    from concourse.bass_utils import run_bass_kernel_spmd

    nc = bacc.Bacc("TRN2", target_bir_lowering=False, num_devices=1)
    arrays = {}

    def given(name, a):
        arrays[name] = np.ascontiguousarray(a)
        return nc.dram_tensor(name, arrays[name].shape, mybir.dt.from_np(arrays[name].dtype), kind="ExternalInput").ap()

    D = x.shape[2]
    DT = D // P
    HC = 512
    w1 = np.concatenate([np.asarray(L0_ffn_shared_w1)[None], np.asarray(L0_ffn_experts_w1)])
    w2 = np.concatenate([np.asarray(L0_ffn_shared_w2)[None], np.asarray(L0_ffn_experts_w2)])
    sets, hidden, _ = w1.shape
    w1 = w1.reshape(sets, hidden // HC, HC, DT, P).transpose(0, 1, 4, 3, 2)
    w2 = w2.reshape(sets, D, hidden // HC, HC // P, P).transpose(0, 2, 4, 3, 1)
    gate_w = np.asarray(L0_ffn_gate_w)
    gamma_media = np.asarray(L0_xattn_gamma_media)
    out = nc.dram_tensor("out", tuple(x.shape), F32, kind="ExternalOutput").ap()
    perceiver_kernel(
        nc,
        x=given("x", np.asarray(x)),
        ctx_in=given("ctx", np.asarray(ctx_1024)),
        mask=given("mask", np.asarray(mask_BxS2_bk0)),
        kv_gate=given("kv_gate", np.asarray(L0_xattn_kv_gate).reshape(1, 1)),
        gamma_media=given("gamma_media", gamma_media.reshape(1, D)),
        beta_media=given("beta_media", np.asarray(L0_xattn_beta_media).reshape(1, D)),
        gamma_media_cols=given("gamma_media_cols", gamma_media.reshape(DT, P).T),
        gamma_lat=given("gamma_lat", np.asarray(L0_xattn_gamma_lat).reshape(1, D)),
        beta_lat=given("beta_lat", np.asarray(L0_xattn_beta_lat).reshape(1, D)),
        wq=given("wq", np.asarray(L0_xattn_Wq)),
        wk_t=given("wk_t", np.asarray(L0_xattn_Wk).T),
        wv=given("wv", np.asarray(L0_xattn_Wv)),
        wout=given("wout", np.asarray(L0_xattn_Wout)),
        w1=given("w1", w1),
        w2=given("w2", w2),
        gate_w_t=given("gate_w_t", gate_w.reshape(gate_w.shape[0], DT, P).transpose(2, 1, 0)),
        kv_latents=nc.dram_tensor("kv_latents", (x.shape[0] * x.shape[1], D), F32, kind="Internal").ap(),
        out=out,
    )
    r = run_bass_kernel_spmd(nc, [arrays], core_ids=[0])
    return r.results[0]["out"]
```
